# Optimizing a Trainium2 kernel written in Bass

```python
import numpy as np
import jax
import jax.numpy as jnp

def _softmax(x, axis=-1):
    return jax.nn.softmax(x, axis=axis)
def _gelu(x):
    return jax.nn.gelu(x, approximate=True)
def _silu(x):
    return jax.nn.silu(x)
def _sigmoid(x):
    return jax.nn.sigmoid(x)
def _layernorm(x, axis=-1, eps=1e-5):
    m = jnp.mean(x, axis=axis, keepdims=True)
    v = jnp.var(x, axis=axis, keepdims=True)
    return (x - m) / jnp.sqrt(v + eps)
def _scatter_add(tgt, idx, src, axis=0):
    return tgt.at[idx].add(src)
def _segment_sum(src, seg, n):
    return jax.ops.segment_sum(src, seg, n)

kernel_name = 'mk_conv_seq_d1_conv_nchw512_dae8b6'

def setup_inputs(seed: int = 0):
    np.random.seed(seed)
    _w = jnp.asarray
    def _rec_inputs():
        import jax
        import jax.numpy as jnp
        _gk = jax.random.key(seed)
        x = 7.22e-05 + 1 * jax.random.normal(jax.random.fold_in(_gk, 1), (16, 512, 32, 32), jnp.float32)
        return x
    x = _rec_inputs()
    def _L0_conv_setup():
        import jax, jax.numpy as jnp
        import numpy as np
        N_HEADS = 8
        key = jax.random.key(seed)
        k1, k2, k3 = jax.random.split(key, 3)
        B, C, H, W = (16, 512, 32, 32)
        x = jax.random.normal(k1, (B, C, H, W), dtype=jnp.float32)
        w_qkv = jax.random.normal(k2, (C, 3 * C), dtype=jnp.float32) * C ** (-0.5)
        b_qkv = jnp.zeros((3 * C,), dtype=jnp.float32)
        w_proj = jax.random.normal(k3, (C, C), dtype=jnp.float32) * C ** (-0.5)
        b_proj = jnp.zeros((C,), dtype=jnp.float32)
        return {'x': x, 'w_qkv': w_qkv, 'b_qkv': b_qkv, 'w_proj': w_proj, 'b_proj': b_proj}
    _L0_conv_all = _L0_conv_setup()
    _L0_conv_in = {k: v for k, v in _L0_conv_all.items() if k in ('w_qkv', 'b_qkv', 'w_proj', 'b_proj', )}
    del _L0_conv_all

    return {
        "x": x,
        "L0_conv_w_qkv": _L0_conv_in["w_qkv"],
        "L0_conv_b_qkv": _L0_conv_in["b_qkv"],
        "L0_conv_w_proj": _L0_conv_in["w_proj"],
        "L0_conv_b_proj": _L0_conv_in["b_proj"],
    }

def reference(x, L0_conv_w_qkv, L0_conv_b_qkv, L0_conv_w_proj, L0_conv_b_proj):
    import jax
    import jax.numpy as jnp
    def _L0_conv_ref(x, w_qkv, b_qkv, w_proj, b_proj):
        import jax, jax.numpy as jnp
        import numpy as np
        N_HEADS = 8
        B, C, H, W = x.shape
        S = H * W
        d_k = C // N_HEADS
        scale = d_k ** (-0.5)
        xr = x.reshape(B, C, S).transpose(0, 2, 1)
        qkv = (xr @ w_qkv + b_qkv).reshape(B, S, N_HEADS, 3 * d_k)
        q, k, v = jnp.split(qkv, 3, axis=-1)
        attn = jnp.einsum('bihd,bjhd->bijh', q, k) * scale
        attn = jax.nn.softmax(attn, axis=2)
        out = jnp.einsum('bijh,bjhd->bihd', attn, v).reshape(B, S, N_HEADS * d_k)
        out = out @ w_proj + b_proj
        out = out.transpose(0, 2, 1).reshape(B, C, H, W)
        return out + x

    def _gn(v, G=32, eps=1e-5):
        B_, C_, H_, W_ = v.shape
        g = v.reshape(B_, G, C_ // G, H_, W_)
        m = jnp.mean(g, axis=(2, 3, 4), keepdims=True)
        s = jnp.var(g, axis=(2, 3, 4), keepdims=True)
        return ((g - m) / jnp.sqrt(s + eps)).reshape(v.shape)

    def _ln_c(v, eps=1e-6):
        m = jnp.mean(v, axis=1, keepdims=True)
        s = jnp.var(v, axis=1, keepdims=True)
        return (v - m) / jnp.sqrt(s + eps)

    def _ln_t(v, eps=1e-5):
        m = jnp.mean(v, axis=-1, keepdims=True)
        s = jnp.var(v, axis=-1, keepdims=True)
        return (v - m) / jnp.sqrt(s + eps)

    def _to_tokens(v):
        B_, C_, H_, W_ = v.shape
        return v.reshape(B_, C_, H_ * W_).transpose(0, 2, 1)
    def _from_tokens(t, like):
        B_, C_, H_, W_ = like.shape
        return t.transpose(0, 2, 1).reshape(B_, C_, H_, W_)

    x = _L0_conv_ref(x, L0_conv_w_qkv, L0_conv_b_qkv, L0_conv_w_proj, L0_conv_b_proj)
    return x


_drawn_inputs = setup_inputs


def setup_inputs(seed=0):
    import zlib

    import numpy as np

    out = dict(_drawn_inputs(seed))
    spreads = {'L0_conv_b_qkv': (0.0, 0.1), 'L0_conv_b_proj': (0.0, 0.1)}
    factors = {}
    for name, (base, spread) in spreads.items():
        noise = np.random.default_rng([zlib.crc32(name.encode()), seed]).standard_normal(out[name].shape)
        drawn = base * np.exp(spread * noise) if base else spread * noise
        out[name] = jnp.asarray(drawn.astype(out[name].dtype))
    for name, factor in factors.items():
        out[name] = (out[name] * factor).astype(out[name].dtype)
    return out
```

```python
import concourse.bass as bass
from concourse import mybir
from contextlib import ExitStack


def attention_kernel(nc, x, w_qkv, b_qkv, w_proj, b_proj, ident, out):
    f32, f32r = mybir.dt.float32, mybir.dt.float32r
    ACT = mybir.ActivationFunctionType
    ALU = mybir.AluOpType
    AXX = mybir.AxisListType.X

    P = 128
    BATCH, C, S = x.shape
    HEADS = 8
    D = C // HEADS
    SCALE = float(D) ** -0.5
    KT = C // P
    NH = 2
    HALF = S // NH
    PAIRS = HEADS // 2
    IT = S // P
    UNITS = HEADS * IT
    QT = IT // NH
    QUARTER = 2 * P
    PVS = UNITS // 2

    PROJECT = {}
    for part in range(2):
        for h in range(1, 7):
            PROJECT[h, part] = ("qk", h + 1, 0, False, part)
            PROJECT[h, 2 + part] = ("qk", h + 1, 1, False, part)
        for h in range(6):
            PROJECT[h, 4 + part] = ("v", h // 2 + 1, h % 2, False, part)
        PROJECT[7, part] = ("qk", 0, 0, True, part)
        PROJECT[7, 2 + part] = ("qk", 0, 1, True, part)
        PROJECT[7, 4 + part] = ("v", 0, 0, True, part)
        PROJECT[7, 6 + part] = ("v", 0, 1, True, part)
    V_TURN = {(h, 7): (h // 2 + 1, h % 2, False) for h in range(6)}
    V_TURN[7, 6] = (0, 0, True)
    V_TURN[0, 0] = (0, 1, False)
    X_CHUNKS = KT * NH
    X_SPLIT = {(6, 4): (0, 1), (6, 5): (2, 3), (6, 6): (4,), (6, 7): (5,), (7, 0): (6,), (7, 1): (7,)}
    NOTHING = ("", 0, 0, False, 0)

    GROUPS0, GROUPS = 6, 32
    QK0, QKS = 4, 2 * HEADS
    V0, VS = 2, 2 * PAIRS
    FILLS0, FILLS = 1, 2 * UNITS + VS
    OUTS = KT * NH
    MOVED = 6 * 16
    LOADS0 = [3, 3, 2]
    LOADS = [6, 5, 5]
    RING = 3

    def x_chunk(b, c):
        k, n = c % KT, c // KT
        return x[b, k * P:(k + 1) * P, n * HALF:(n + 1) * HALF]

    def tile_of(t, b, g):
        n, m = g // KT, g % KT
        return t[b, m * P:(m + 1) * P, n * HALF:(n + 1) * HALF]

    ctx = ExitStack()
    with ctx:
        def sb(name, shape, dt=f32):
            return ctx.enter_context(nc.sbuf_tensor(name, shape, dt))

        def sem(name):
            return ctx.enter_context(nc.semaphore(name))

        wqk = [sb(f"wqk_{s}", [P, KT, HEADS, P], f32r) for s in "hl"]
        wv = [sb(f"wv_{s}", [P, KT, HEADS, D], f32r) for s in "hl"]
        wp = [sb(f"wp_{s}", [P, KT, C], f32r) for s in "hl"]
        xs = [sb(f"x_{s}", [P, KT, S], f32r) for s in "hl"]
        q_hl = [sb(f"q_hl{i}", [P, S], f32r) for i in range(2)]
        k_hh = [sb(f"k_hh{i}", [P, S], f32r) for i in range(2)]
        k_ll = [sb(f"k_ll{i}", [P, S], f32r) for i in range(2)]
        v_hl = [sb(f"v_hl{i}", [P, IT, 2, P], f32r) for i in range(2)]
        pt = [sb(f"pt_{s}", [P, 2, IT, QUARTER], f32r) for s in "hl"]
        os_ = [t[:].rearrange("p i a b -> p (i a b)").rearrange("p (k s) -> p k s", k=KT) for t in pt]
        probs = [sb(f"probs{i}", [P, S]) for i in range(2)]
        o = sb("o", [P, PAIRS, S])
        stage_qk = [sb(f"stage_qk_{s}", [P, HALF], f32r) for s in "hl"]
        v_t = sb("v_t", [P, HALF])
        o_low = sb("o_low", [D, HALF])
        ring = [sb(f"ring{i}", [P, HALF]) for i in range(RING)]
        idm = sb("idm", [P, P])
        bqk = sb("bqk", [P, HEADS])
        bv = sb("bv", [P, PAIRS])
        bp = sb("bp", [P, KT])
        negmax = sb("negmax", [P, 2])
        sums = sb("sums", [P, 2])
        rinv = sb("rinv", [P, 2])
        w_stage = o[:].rearrange("p a b -> p (a b)").rearrange("p (i n) -> p i n", i=2)

        scores = [ctx.enter_context(nc.psum_tensor(f"scores{i}", [P, S], f32)) for i in range(2)]
        turned = [ctx.enter_context(nc.psum_tensor(f"turned{i}", [P, 4, P], f32)) for i in range(2)]
        ps_o = ctx.enter_context(nc.psum_tensor("ps_o", [P, HALF], f32))
        ps_g = ctx.enter_context(nc.psum_tensor("ps_g", [P, HALF], f32))

        const_loaded = sem("const_loaded")
        w_loaded = [sem(f"w_loaded{i}") for i in range(2)]
        w_high = sem("w_high")
        w_low = sem("w_low")
        b_scaled = sem("b_scaled")
        ring_loaded = [sem(f"ring_loaded{i}") for i in range(RING)]
        x_high = sem("x_high")
        x_low = sem("x_low")
        group_done = sem("group_done")
        qk_high = sem("qk_high")
        qk_low = sem("qk_low")
        qk_moved = sem("qk_moved")
        vt_done = sem("vt_done")
        scores_done = sem("scores_done")
        max_done = sem("max_done")
        exp_done = sem("exp_done")
        recip_done = sem("recip_done")
        norm_done = sem("norm_done")
        fill_done = sem("fill_done")
        fill_high = sem("fill_high")
        fill_low = sem("fill_low")
        pv_done = sem("pv_done")
        olow_done = sem("olow_done")
        o_done = sem("o_done")
        os_high = sem("os_high")
        os_low = sem("os_low")
        out_done = sem("out_done")
        stored = sem("stored")

        block = ctx.enter_context(nc.Block())

        @block.sync
        def _(sp):
            def move_qk(head, n, nqk):
                cols = slice(n * HALF, (n + 1) * HALF)
                i = head % 2
                sp.wait_ge(qk_low, nqk + 1)
                hi, lo = (s[:].bitcast(f32) for s in stage_qk)
                for dst, rows, src in ((q_hl[i], 0, hi[0:D]), (q_hl[i], D, lo[0:D]),
                                       (k_hh[i], 0, hi[D:P]), (k_hh[i], D, hi[D:P]),
                                       (k_ll[i], 0, lo[D:P]), (k_ll[i], D, lo[D:P])):
                    sp.dma_start(dst[rows:rows + D, cols].bitcast(f32), src).then_inc(qk_moved, 16)

            sp.sem_inc(stored, 16)
            for c in range(RING):
                sp.dma_start(ring[c][:], x_chunk(0, c)).then_inc(ring_loaded[c], 16)
            sp.dma_start(w_stage[:, 0, 0:3 * C], w_qkv[0:P, :]).then_inc(w_loaded[0], 16)
            sp.dma_start(w_stage[:, 1, 0:3 * C], w_qkv[P:2 * P, :]).then_inc(w_loaded[1], 16)
            sp.dma_start(idm[:], ident).then_inc(const_loaded, 16)
            bq = b_qkv.rearrange("(h c) -> c h", c=3 * D)
            sp.dma_start(bqk[:], bq[0:P, :], allow_slow_non_contiguous=True).then_inc(const_loaded, 16)
            bvv = b_qkv.rearrange("(k a c) -> a c k", a=2, c=3 * D)
            for a in range(2):
                sp.dma_start(bv[a * D:(a + 1) * D, :], bvv[a, 2 * D:3 * D, :],
                             allow_slow_non_contiguous=True).then_inc(const_loaded, 16)
            sp.dma_start(bp[:], b_proj.rearrange("(m c) -> c m", c=P),
                         allow_slow_non_contiguous=True).then_inc(const_loaded, 16)
            for c in range(RING, X_CHUNKS):
                sp.wait_ge(x_low, c - RING + 1)
                sp.dma_start(ring[c % RING][:], x_chunk(0, c)).then_inc(ring_loaded[c % RING], 16)
            for k in range(2, KT):
                sp.wait_ge(w_low, 3 * (k - 1))
                sp.dma_start(w_stage[:, k % 2, 0:3 * C],
                             w_qkv[k * P:(k + 1) * P, :]).then_inc(w_loaded[k % 2], 16)
            for k in range(0, KT, 2):
                sp.wait_ge(w_low, 3 * KT if k else 3 * (KT - 1))
                sp.dma_start(w_stage[:, k // 2, 0:2 * C].rearrange("p (k n) -> p k n", k=2),
                             w_proj[k * P:(k + 2) * P, :].rearrange("(k p) n -> p k n", p=P)
                             ).then_inc(w_loaded[k // 2], 16)
            for head in range(2):
                for n in range(NH):
                    move_qk(head, n, 2 * head + n)

            def body(b, more):
                nqk = QKS * b + QK0
                step = 0
                loads = list(LOADS0)
                for h in range(HEADS):
                    for t in range(IT):
                        kind, head, n, ahead, part = PROJECT.get((h, t), NOTHING)
                        if kind == "qk" and part and (more or not ahead):
                            move_qk(head, n, nqk + step)
                            step += 1
                        if more and (h, t) == (6, 3):
                            sp.wait_ge(stored, 16 * OUTS * b + 16)
                            for c in range(X_CHUNKS):
                                free = X_CHUNKS * b + (X_CHUNKS + max(c - RING + 1, 0))
                                sp.wait_ge(x_low, free)
                                sp.dma_start(ring[c % RING][:], x_chunk(b + 1, c)
                                             ).then_inc(ring_loaded[c % RING], 16)
                if more:
                    sp.wait_ge(x_low, X_CHUNKS * b + 2 * X_CHUNKS)
                else:
                    sp.wait_ge(stored, 16 * OUTS * b + 16)
                for g in range(RING):
                    i = (X_CHUNKS + g) % RING
                    sp.dma_start(ring[i][:], tile_of(x, b, g)).then_inc(ring_loaded[i], 16)
                if more:
                    for n in range(NH):
                        move_qk(1, n, nqk + step)
                        step += 1
                for g in range(OUTS):
                    i = (X_CHUNKS + g) % RING
                    sp.wait_ge(out_done, OUTS * b + (g + 2))
                    sp.dma_start(tile_of(out, b, g), ring[i][:]).then_inc(stored, 16)
                    if g + RING < OUTS:
                        sp.wait_ge(stored, 16 * OUTS * b + 16 * (g + 2))
                        sp.dma_start(ring[i][:], tile_of(x, b, g + RING)).then_inc(ring_loaded[i], 16)

            with sp.Fori(0, BATCH - 1) as b:
                body(b, True)
            body(BATCH - 1, False)
            sp.wait_ge(stored, 16 * OUTS * BATCH + 16)

        @block.tensor
        def _(pe):
            def product(bank, w, w_col, r, r_col, part):
                terms = [(k, i, j) for k in range(KT) for i, j in ((0, 0), (0, 1), (1, 0))]
                half = len(terms) // 2
                for e, (k, i, j) in enumerate(terms):
                    if part is not None and e // half != part:
                        continue
                    last = nc.tensor.matmul(bank[:], w_col(w[i], k), r_col(r[j], k),
                                            start=e == 0, stop=e == len(terms) - 1)
                return last

            def project_qk(bank, head, n, part=None):
                return product(bank, wqk, lambda w, k: w[:, k, head, :],
                               xs, lambda a, k: a[:, k, n * HALF:(n + 1) * HALF], part)

            def project_v(bank, pair, n, part=None):
                return product(bank, wv, lambda w, k: w[:, k, 2 * pair:2 * pair + 2, :],
                               xs, lambda a, k: a[:, k, n * HALF:(n + 1) * HALF], part)

            def project_out(bank, g):
                n, m = g // KT, g % KT
                return product(bank, wp, lambda w, k: w[:, k, m * P:(m + 1) * P],
                               os_, lambda a, k: a[:, k, n * HALF:(n + 1) * HALF], None)

            def score(u):
                head, it = u // IT, u % IT
                i = head % 2
                for n in range(NH):
                    for e, kk in enumerate((k_hh, k_ll)):
                        last = nc.tensor.matmul(scores[u % 2][:, n * HALF:(n + 1) * HALF],
                                                q_hl[i][:, it * P:(it + 1) * P],
                                                kk[i][:, n * HALF:(n + 1) * HALF],
                                                start=e == 0, stop=e == 1)
                return last

            def turn(bank, blocks):
                for j, blk in enumerate(blocks):
                    last = nc.tensor.transpose(turned[bank][:, j, :], blk, idm[:])
                return last

            pe.wait_ge(w_low, 3 * KT)
            for i in range(4):
                pe.wait_ge(x_low, KT * (i % 2 + 1))
                if i > 0:
                    pe.wait_ge(qk_low, i)
                project_qk(ps_g, i // 2, i % 2).then_inc(group_done, 1)
            pe.wait_ge(const_loaded, 16 * 5)
            for n in range(NH):
                if n == 0:
                    pe.wait_ge(qk_low, QK0)
                else:
                    pe.wait_ge(vt_done, n)
                project_v(ps_g, 0, n).then_inc(group_done, 1)
                if n == 0:
                    pe.wait_ge(vt_done, n + 1)
                    turn(0, [v_t[:, j * P:(j + 1) * P] for j in range(QT)]).then_inc(fill_done, 1)
            pe.wait_ge(qk_moved, MOVED * QK0)
            for u in range(2):
                score(u).then_inc(scores_done, 1)

            def body(b, more):
                fill, nqk, nv = FILLS0, QK0, V0
                last_g = "out"

                def g_free():
                    if last_g == "qk":
                        pe.wait_ge(qk_low, QKS * b + nqk)
                    elif last_g == "v":
                        pe.wait_ge(vt_done, VS * b + nv)
                    else:
                        pe.wait_ge(out_done, OUTS * b + 1)
                        pe.wait_ge(qk_low, QKS * b + nqk)
                        pe.wait_ge(vt_done, VS * b + nv)

                def attend(q, part, fills):
                    head, quarter = q // (IT // 2), q % (IT // 2)
                    cols = slice((quarter % 2) * QUARTER, (quarter % 2 + 1) * QUARTER)
                    if part == 0:
                        pe.wait_ge(fill_low, FILLS * b + fills)
                        if q == 0:
                            pe.wait_ge(out_done, OUTS * b + 1)
                        elif q % 2 == 0:
                            pe.wait_ge(o_done, 2 * HEADS * b + q // 2)
                    for jt in range(QT * part, QT * (part + 1)):
                        for e in range(2):
                            last = nc.tensor.matmul(ps_o[:, cols], v_hl[head // 2 % 2][:, jt, head % 2, :],
                                                    pt[e][:, q % 2, jt, :],
                                                    start=jt == 0 and e == 0, stop=jt == IT - 1 and e == 1)
                    if part:
                        last.then_inc(pv_done, 1)

                for h in range(HEADS):
                    for t in range(IT):
                        u = h * IT + t
                        before = fill
                        if more or u + 2 < UNITS:
                            nxt = (u + 2) % UNITS
                            pe.wait_ge(exp_done, UNITS * b + (u + 1))
                            if nxt % IT == 0:
                                pe.wait_ge(qk_moved, MOVED * QKS * b + MOVED * nqk)
                            score(nxt).then_inc(scores_done, 1)
                        pe.wait_ge(norm_done, UNITS * b + (u + 1))
                        for f in range(2):
                            pe.wait_ge(fill_low, FILLS * b + max(fill - 1, 1))
                            turn(fill % 2, [probs[u % 2][:, j * P:(j + 1) * P]
                                            for j in range(QT * f, QT * (f + 1))]).then_inc(fill_done, 1)
                            fill += 1
                        if u >= 2:
                            attend(u // 2 - 1, u % 2, before)
                        kind, head, n, ahead, part = PROJECT.get((h, t), NOTHING)
                        if kind and (more or not ahead):
                            if part == 0:
                                g_free()
                            if kind == "qk":
                                if ahead and part == 0:
                                    pe.wait_ge(x_low, X_CHUNKS * b + (X_CHUNKS + KT * (n + 1)))
                                last = project_qk(ps_g, head, n, part)
                            else:
                                last = project_v(ps_g, head, n, part)
                            if part:
                                last.then_inc(group_done, 1)
                                nqk += kind == "qk"
                                nv += kind == "v"
                                last_g = kind
                        if (h, t) in V_TURN and (more or not V_TURN[h, t][2]):
                            pe.wait_ge(fill_low, FILLS * b + (fill - 1))
                            pe.wait_ge(vt_done, VS * b + nv)
                            turn(fill % 2, [v_t[:, j * P:(j + 1) * P] for j in range(QT)]
                                 ).then_inc(fill_done, 1)
                            fill += 1
                for part in range(2):
                    attend(PVS - 1, part, fill)
                if more:
                    for n in range(NH):
                        g_free()
                        project_qk(ps_g, 1, n).then_inc(group_done, 1)
                        nqk += 1
                        last_g = "qk"
                if not more:
                    pe.wait_ge(w_low, 3 * KT + 2)
                for g in range(OUTS):
                    n = g // KT
                    if g % KT == 0:
                        pe.wait_ge(os_low, 2 * KT * b + KT * (n + 1))
                    if g == 0:
                        pe.wait_ge(o_done, 2 * HEADS * b + 2 * HEADS)
                        pe.wait_ge(w_low, 3 * KT + 2)
                    elif g == 1:
                        g_free()
                    else:
                        pe.wait_ge(out_done, OUTS * b + g)
                    project_out(ps_o if g % 2 == 0 else ps_g, g).then_inc(group_done, 1)

            with pe.Fori(0, BATCH - 1) as b:
                body(b, True)
            body(BATCH - 1, False)

        @block.scalar
        def _(act):
            def exponentials(u, unit):
                act.wait_ge(max_done, unit + 1)
                nc.scalar.activation(probs[u % 2][:], scores[u % 2][:], ACT.Exp, bias=negmax[:, u % 2:u % 2 + 1],
                                     scale=1.0, accum_out=sums[:, u % 2:u % 2 + 1]).then_inc(exp_done, 1)

            def stage_high(head):
                nc.scalar.activation(stage_qk[0][:], ps_g[:], ACT.Identity,
                                     bias=bqk[:, head:head + 1], scale=1.0).then_inc(qk_high, 1)

            def stage_v(pair):
                nc.scalar.activation(v_t[:], ps_g[:], ACT.Identity,
                                     bias=bv[:, pair:pair + 1], scale=1.0).then_inc(vt_done, 1)

            def split_x(c, slot):
                k, n = c % KT, c // KT
                nc.scalar.activation(xs[0][:, k, n * HALF:(n + 1) * HALF], ring[slot][:],
                                     ACT.Copy).then_inc(x_high, 1)

            def v_high(pair, n, bank):
                nc.scalar.activation(v_hl[pair % 2][:, QT * n:QT * (n + 1), :, 0:D],
                                     turned[bank][:].rearrange("p j (a d) -> p j a d", a=2),
                                     ACT.Copy).then_inc(fill_high, 1)

            for c in range(RING):
                act.wait_ge(ring_loaded[c], 16)
                split_x(c, c)
            for k in range(KT):
                act.wait_ge(w_loaded[k % 2], 16 * (k // 2 + 1))
                for part, (dst, scale) in enumerate(((wqk[0][:, k, :, 0:D], SCALE), (wqk[0][:, k, :, D:P], 1.0),
                                                     (wv[0][:, k, :, :], 1.0))):
                    src = w_stage[:, k % 2, 0:3 * C].rearrange("p (h c) -> p h c", h=HEADS)
                    nc.scalar.activation(dst, src[:, :, part * D:(part + 1) * D], ACT.Copy,
                                         scale=scale).then_inc(w_high, 1)
                if k < 2:
                    for c in range(RING + 3 * k, min(RING + 3 * k + 3, X_CHUNKS)):
                        act.wait_ge(ring_loaded[c % RING], 16 * (c // RING + 1))
                        split_x(c, c % RING)
            act.wait_ge(b_scaled, 1)
            for i in range(QK0):
                act.wait_ge(group_done, i + 1)
                if i > 0:
                    act.wait_ge(qk_moved, MOVED * i)
                stage_high(i // 2)
            for n in range(NH):
                act.wait_ge(group_done, QK0 + n + 1)
                if n:
                    act.wait_ge(fill_done, n)
                stage_v(0)
                if n == 0:
                    act.wait_ge(fill_done, 1)
                    v_high(0, 0, 0)
            for i in range(2):
                act.wait_ge(w_loaded[i], 16 * 3)
                nc.scalar.activation(wp[0][:, 2 * i:2 * i + 2, :],
                                     w_stage[:, i, 0:2 * C].rearrange("p (k n) -> p k n", k=2),
                                     ACT.Copy).then_inc(w_high, 1)
            for u in range(2):
                exponentials(u, u)

            def body(b, more):
                fill, group, nqk, nv = FILLS0, GROUPS0, QK0, V0
                loads = list(LOADS0)

                def lower_half_out(half_index):
                    act.wait_ge(pv_done, PVS * b + 2 * (half_index + 1))
                    if half_index:
                        act.wait_ge(o_done, 2 * HEADS * b + half_index)
                    nc.scalar.copy(o_low[:], ps_o[D:P, :]).then_inc(olow_done, 1)

                for h in range(HEADS):
                    for t in range(IT):
                        u = h * IT + t
                        for f in range(2):
                            act.wait_ge(fill_done, FILLS * b + (fill + 1))
                            if u == 0 and f == 0:
                                act.wait_ge(group_done, GROUPS * b + GROUPS0)
                            elif u % 2 == 0 and u >= 4 and f == 0:
                                act.wait_ge(pv_done, PVS * b + (u // 2 - 1))
                            col = (u % 2) * P
                            nc.scalar.activation(pt[0][:, u // 2 % 2, QT * f:QT * (f + 1), col:col + P],
                                                 turned[fill % 2][:],
                                                 ACT.Copy).then_inc(fill_high, 1)
                            fill += 1
                        if more or u + 2 < UNITS:
                            exponentials(u, UNITS * b + (u + 2))
                        kind, head, n, ahead, part = PROJECT.get((h, t), NOTHING)
                        if u % 4 == 1 and u >= 5:
                            lower_half_out((u - 5) // 4)
                        if kind and part and (more or not ahead):
                            group += 1
                            act.wait_ge(group_done, GROUPS * b + group)
                            if kind == "qk":
                                act.wait_ge(qk_moved, MOVED * QKS * b + MOVED * nqk)
                                stage_high(head)
                                nqk += 1
                            else:
                                act.wait_ge(fill_done, FILLS * b + fill)
                                stage_v(head)
                        if (h, t) in V_TURN and (more or not V_TURN[h, t][2]):
                            act.wait_ge(fill_done, FILLS * b + (fill + 1))
                            v_high(V_TURN[h, t][0], V_TURN[h, t][1], fill % 2)
                            fill += 1
                        for c in X_SPLIT.get((h, t), ()) if more else ():
                            slot = c % RING
                            loads[slot] += 1
                            act.wait_ge(ring_loaded[slot], 16 * LOADS[slot] * b + 16 * loads[slot])
                            split_x(c, slot)
                lower_half_out(2 * HEADS - 1)
                for n in range(NH):
                    for k in range(KT):
                        if k == 2 and more:
                            group += 1
                            act.wait_ge(group_done, GROUPS * b + group)
                            act.wait_ge(qk_moved, MOVED * QKS * b + MOVED * nqk)
                            stage_high(1)
                            nqk += 1
                        if k == KT - 1 and n == 0:
                            act.wait_ge(o_done, 2 * HEADS * b + 2 * HEADS)
                        nc.scalar.activation(os_[0][:, k, n * HALF:(n + 1) * HALF], o[:, k, n * HALF:(n + 1) * HALF],
                                             ACT.Copy).then_inc(os_high, 1)

            with act.Fori(0, BATCH - 1) as b:
                body(b, True)
            body(BATCH - 1, False)

        @block.vector
        def _(dve):
            def maximum(u, unit):
                dve.wait_ge(scores_done, unit + 1)
                nc.vector.tensor_reduce(negmax[:, u % 2:u % 2 + 1], scores[u % 2][:], AXX, ALU.max,
                                        negate=True).then_inc(max_done, 1)

            def reciprocal(u, unit):
                dve.wait_ge(exp_done, unit + 1)
                nc.vector.reciprocal(rinv[:, u % 2:u % 2 + 1], sums[:, u % 2:u % 2 + 1]).then_inc(recip_done, 1)

            def stage_low(head):
                nc.vector.scalar_tensor_tensor(out=stage_qk[1][:], in0=ps_g[:], scalar=bqk[:, head:head + 1],
                                               in1=stage_qk[0][:].bitcast(f32), op0=ALU.add,
                                               op1=ALU.subtract).then_inc(qk_low, 1)

            def v_low(pair, n, bank):
                v = v_hl[pair % 2][:, QT * n:QT * (n + 1), :, :]
                nc.vector.tensor_tensor(v[:, :, :, D:P], turned[bank][:].rearrange("p j (a d) -> p j a d", a=2),
                                        v[:, :, :, 0:D].bitcast(f32), ALU.subtract).then_inc(fill_low, 1)

            dve.wait_ge(const_loaded, 16 * 5)
            nc.vector.tensor_scalar(bqk[0:D, :], bqk[0:D, :], SCALE, None, ALU.mult).then_inc(b_scaled, 1)
            nc.vector.memset(rinv[:], 0.0).then_inc(out_done, 1)
            for k in range(KT):
                src = w_stage[:, k % 2, 0:3 * C].rearrange("p (h c) -> p h c", h=HEADS)
                for part, (hi, lo, scale) in enumerate(
                        ((wqk[0][:, k, :, 0:D], wqk[1][:, k, :, 0:D], SCALE),
                         (wqk[0][:, k, :, D:P], wqk[1][:, k, :, D:P], 1.0),
                         (wv[0][:, k, :, :], wv[1][:, k, :, :], 1.0))):
                    dve.wait_ge(w_high, 3 * k + part + 1)
                    nc.vector.scalar_tensor_tensor(out=lo, in0=src[:, :, part * D:(part + 1) * D], scalar=scale,
                                                   in1=hi.bitcast(f32), op0=ALU.mult,
                                                   op1=ALU.subtract).then_inc(w_low, 1)
            dve.wait_ge(b_scaled, 1)
            for i in range(QK0):
                dve.wait_ge(qk_high, i + 1)
                stage_low(i // 2)
            dve.wait_ge(fill_high, 1)
            v_low(0, 0, 0)
            for i in range(2):
                dve.wait_ge(w_high, 3 * KT + i + 1)
                nc.vector.tensor_tensor(wp[1][:, 2 * i:2 * i + 2, :],
                                        w_stage[:, i, 0:2 * C].rearrange("p (k n) -> p k n", k=2),
                                        wp[0][:, 2 * i:2 * i + 2, :].bitcast(f32),
                                        ALU.subtract).then_inc(w_low, 1)
            for u in range(2):
                maximum(u, u)
            for u in range(2):
                reciprocal(u, u)

            def body(b, more):
                fill, nqk = FILLS0, QK0
                loads = list(LOADS0)

                def whole_out(half_index):
                    head, half = half_index // 2, half_index % 2
                    rows = slice((head % 2) * D, (head % 2 + 1) * D)
                    dve.wait_ge(olow_done, 2 * HEADS * b + (half_index + 1))
                    nc.vector.tensor_tensor(o[rows, head // 2, half * HALF:(half + 1) * HALF], ps_o[0:D, :],
                                            o_low[:], ALU.add).then_inc(o_done, 1)

                for h in range(HEADS):
                    for t in range(IT):
                        u = h * IT + t
                        ahead_unit = more or u + 2 < UNITS
                        if ahead_unit:
                            maximum(u, UNITS * b + (u + 2))
                        for f in range(2):
                            dve.wait_ge(fill_high, FILLS * b + (fill + 1))
                            part = (slice(None), u // 2 % 2, slice(QT * f, QT * (f + 1)),
                                    slice((u % 2) * P, (u % 2 + 1) * P))
                            nc.vector.tensor_tensor(pt[1][part], turned[fill % 2][:], pt[0][part].bitcast(f32),
                                                    ALU.subtract).then_inc(fill_low, 1)
                            fill += 1
                        if ahead_unit:
                            reciprocal(u, UNITS * b + (u + 2))
                        kind, head, n, ahead, part = PROJECT.get((h, t), NOTHING)
                        if u % 4 == 1 and u >= 5:
                            whole_out((u - 5) // 4)
                        if kind == "qk" and part and (more or not ahead):
                            nqk += 1
                            dve.wait_ge(qk_high, QKS * b + nqk)
                            stage_low(head)
                        if (h, t) in V_TURN and (more or not V_TURN[h, t][2]):
                            dve.wait_ge(fill_high, FILLS * b + (fill + 1))
                            v_low(V_TURN[h, t][0], V_TURN[h, t][1], fill % 2)
                            fill += 1
                        for c in X_SPLIT.get((h, t), ()) if more else ():
                            loads[c % RING] += 1
                whole_out(2 * HEADS - 1)
                for n in range(NH):
                    for k in range(KT):
                        if k == 2 and more:
                            nqk += 1
                            dve.wait_ge(qk_high, QKS * b + nqk)
                            stage_low(1)
                        dve.wait_ge(os_high, 2 * KT * b + (KT * n + k + 1))
                        src = o[:, k, n * HALF:(n + 1) * HALF]
                        if k == KT - 1 and n == 0:
                            dve.wait_ge(o_done, 2 * HEADS * b + 2 * HEADS)
                        nc.vector.tensor_tensor(os_[1][:, k, n * HALF:(n + 1) * HALF], src,
                                                os_[0][:, k, n * HALF:(n + 1) * HALF].bitcast(f32),
                                                ALU.subtract).then_inc(os_low, 1)
                for g in range(OUTS):
                    slot = (X_CHUNKS + g) % RING
                    loads[slot] += 1
                    group = GROUPS0 + (GROUPS - OUTS) - (0 if more else 6) + g + 1
                    dve.wait_ge(group_done, GROUPS * b + group)
                    dve.wait_ge(ring_loaded[slot], 16 * LOADS[slot] * b + 16 * loads[slot])
                    nc.vector.scalar_tensor_tensor(out=ring[slot][:], in0=(ps_o if g % 2 == 0 else ps_g)[:],
                                                   scalar=bp[:, g % KT:g % KT + 1], in1=ring[slot][:],
                                                   op0=ALU.add, op1=ALU.add).then_inc(out_done, 1)

            with dve.Fori(0, BATCH - 1) as b:
                body(b, True)
            body(BATCH - 1, False)

        @block.gpsimd
        def _(pool):
            def split_x(c, slot):
                k, n = c % KT, c // KT
                cols = slice(n * HALF, (n + 1) * HALF)
                nc.gpsimd.tensor_tensor(xs[1][:, k, cols], ring[slot][:], xs[0][:, k, cols].bitcast(f32),
                                        ALU.subtract).then_inc(x_low, 1)

            def normalise(u, unit):
                pool.wait_ge(recip_done, unit + 1)
                nc.gpsimd.tensor_tensor(probs[u % 2][:], probs[u % 2][:],
                                        rinv[:, u % 2:u % 2 + 1].broadcast_to([P, S]),
                                        ALU.mult).then_inc(norm_done, 1)

            for c in range(X_CHUNKS):
                pool.wait_ge(x_high, c + 1)
                split_x(c, c % RING)
            for u in range(2):
                normalise(u, u)

            def body(b, more):
                for h in range(HEADS):
                    for t in range(IT):
                        u = h * IT + t
                        if more or u + 2 < UNITS:
                            normalise(u, UNITS * b + (u + 2))
                        for c in X_SPLIT.get((h, t), ()) if more else ():
                            pool.wait_ge(x_high, X_CHUNKS * b + (X_CHUNKS + c + 1))
                            split_x(c, c % RING)

            with pool.Fori(0, BATCH - 1) as b:
                body(b, True)
            body(BATCH - 1, False)


def kernel(x, L0_conv_w_qkv, L0_conv_b_qkv, L0_conv_w_proj, L0_conv_b_proj):
    import numpy as np
    import concourse.bacc as bacc
    from concourse.bass_utils import run_bass_kernel_spmd

    x = np.asarray(x)
    batch, channels, height, width = x.shape
    arrays = {
        "x_in": np.ascontiguousarray(x).reshape(batch, channels, height * width),
        "w_qkv_in": np.ascontiguousarray(L0_conv_w_qkv),
        "b_qkv_in": np.ascontiguousarray(L0_conv_b_qkv),
        "w_proj_in": np.ascontiguousarray(L0_conv_w_proj),
        "b_proj_in": np.ascontiguousarray(L0_conv_b_proj),
        "ident_in": np.eye(128, dtype=np.float32),
    }
    nc = bacc.Bacc("TRN2", target_bir_lowering=False, num_devices=1)
    ins = [nc.dram_tensor(n, a.shape, mybir.dt.from_np(a.dtype), kind="ExternalInput").ap()
           for n, a in arrays.items()]
    out = nc.dram_tensor("out", arrays["x_in"].shape, mybir.dt.float32, kind="ExternalOutput").ap()
    attention_kernel(nc, *ins, out)
    result = run_bass_kernel_spmd(nc, [arrays], core_ids=[0])
    return result.results[0]["out"].reshape(x.shape)
```

```python
import concourse.bass as bass
from concourse import mybir
from contextlib import ExitStack


def attention_kernel(nc, x, w_qkv, b_qkv, w_proj, b_proj, ident, out):
    f32, f32r = mybir.dt.float32, mybir.dt.float32r
    ACT = mybir.ActivationFunctionType
    ALU = mybir.AluOpType
    AXX = mybir.AxisListType.X

    P = 128
    BATCH, C, S = x.shape
    HEADS = 8
    D = C // HEADS
    SCALE = float(D) ** -0.5
    KT = C // P
    NH = 2
    HALF = S // NH
    PAIRS = HEADS // 2
    IT = S // P
    UNITS = HEADS * IT
    QT = IT // NH
    QUARTER = 2 * P
    PVS = UNITS // 2

    PROJECT = {}
    for part in range(2):
        for h in range(1, 7):
            PROJECT[h, part] = ("qk", h + 1, 0, False, part, 2)
            PROJECT[h, 2 + part] = ("qk", h + 1, 1, False, part, 2)
        PROJECT[7, part] = ("qk", 0, 0, True, part, 2)
        PROJECT[7, 2 + part] = ("qk", 0, 1, True, part, 2)
        PROJECT[7, 4 + part] = ("v", 0, 0, True, part, 2)
        PROJECT[7, 6 + part] = ("v", 0, 1, True, part, 2)
    for part in range(4):
        for h in range(6):
            PROJECT[h, part + (4 if h else 0)] = ("v", h // 2 + 1, h % 2, False, part, 4)
    V_TURN = {(h + 1, 0): (h // 2 + 1, h % 2, False) for h in range(6)}
    V_TURN[7, 6] = (0, 0, True)
    V_TURN[0, 2] = (0, 1, False)
    X_CHUNKS = KT * NH
    X_SPLIT = {(6, 2): (0, 1), (6, 3): (2,), (6, 4): (3,), (6, 5): (4,), (6, 6): (5,), (6, 7): (6,), (7, 0): (7,)}
    X_LOAD = {(1, 3): range(5), (6, 3): range(5, X_CHUNKS)}
    NOTHING = ("", 0, 0, False, 0, 1)

    GROUPS0, GROUPS = 6, 32
    QK0, QKS = 4, 2 * HEADS
    V0, VS = 2, 2 * PAIRS
    FILLS0, FILLS = 1, 2 * UNITS + VS
    OUTS = KT * NH
    COPIED = 2 * 16
    RING = 5
    SLOT_OF = [i % RING for i in range(X_CHUNKS + OUTS)]
    LOADS0 = [SLOT_OF[:X_CHUNKS].count(i) for i in range(RING)]
    LOADS = [SLOT_OF.count(i) for i in range(RING)]

    def x_chunk(b, c):
        k, n = c % KT, c // KT
        return x[b, k * P:(k + 1) * P, n * HALF:(n + 1) * HALF]

    def tile_of(t, b, g):
        n, m = g // KT, g % KT
        return t[b, m * P:(m + 1) * P, n * HALF:(n + 1) * HALF]

    ctx = ExitStack()
    with ctx:
        def sb(name, shape, dt=f32):
            return ctx.enter_context(nc.sbuf_tensor(name, shape, dt))

        def sem(name):
            return ctx.enter_context(nc.semaphore(name))

        wqk = [sb(f"wqk_{s}", [P, KT, HEADS, P], f32r) for s in "hl"]
        wv = [sb(f"wv_{s}", [P, KT, HEADS, D], f32r) for s in "hl"]
        wp = [sb(f"wp_{s}", [P, KT, C], f32r) for s in "hl"]
        xs = [sb(f"x_{s}", [P, KT, S], f32r) for s in "hl"]
        q_hl = [sb(f"q_hl{i}", [P, S], f32r) for i in range(2)]
        k_hh = [sb(f"k_hh{i}", [P, S], f32r) for i in range(2)]
        k_ll = [sb(f"k_ll{i}", [P, S], f32r) for i in range(2)]
        v_hl = [sb(f"v_hl{i}", [P, IT, 2, P], f32r) for i in range(2)]
        pt = [sb(f"pt_{s}", [P, 2, IT, QUARTER], f32r) for s in "hl"]
        os_ = [t[:].rearrange("p i a b -> p (i a b)").rearrange("p (k s) -> p k s", k=KT) for t in pt]
        probs = [sb(f"probs{i}", [P, S]) for i in range(2)]
        o = sb("o", [P, PAIRS, S])
        v_t = sb("v_t", [P, HALF])
        o_low = sb("o_low", [D, HALF])
        ring = [sb(f"ring{i}", [P, HALF]) for i in range(RING)]
        idm = sb("idm", [P, P])
        bqk = sb("bqk", [P, HEADS])
        bv = sb("bv", [P, PAIRS])
        bp = sb("bp", [P, KT])
        negmax = sb("negmax", [P, 2])
        sums = sb("sums", [P, 2])
        rinv = sb("rinv", [P, 2])
        w_stage = o[:].rearrange("p a b -> p (a b)").rearrange("p (i n) -> p i n", i=2)

        scores = [ctx.enter_context(nc.psum_tensor(f"scores{i}", [P, S], f32)) for i in range(2)]
        turned = [ctx.enter_context(nc.psum_tensor(f"turned{i}", [P, 4, P], f32)) for i in range(2)]
        turned_flat = turned[(FILLS0 + FILLS) % 2][:].rearrange("p j c -> p (j c)")
        ps_o = ctx.enter_context(nc.psum_tensor("ps_o", [P, HALF], f32))
        ps_g = ctx.enter_context(nc.psum_tensor("ps_g", [P, HALF], f32))

        const_loaded = sem("const_loaded")
        w_loaded = [sem(f"w_loaded{i}") for i in range(2)]
        w_high = sem("w_high")
        w_low = sem("w_low")
        b_scaled = sem("b_scaled")
        ring_loaded = [sem(f"ring_loaded{i}") for i in range(RING)]
        x_high = sem("x_high")
        x_low = sem("x_low")
        group_done = sem("group_done")
        qk_high = sem("qk_high")
        qk_low = sem("qk_low")
        qk_copied = sem("qk_copied")
        vt_done = sem("vt_done")
        scores_done = sem("scores_done")
        max_done = sem("max_done")
        exp_done = sem("exp_done")
        recip_done = sem("recip_done")
        norm_done = sem("norm_done")
        fill_done = sem("fill_done")
        fill_high = sem("fill_high")
        fill_low = sem("fill_low")
        pv_done = sem("pv_done")
        olow_done = sem("olow_done")
        o_done = sem("o_done")
        os_high = sem("os_high")
        os_low = sem("os_low")
        out_done = sem("out_done")
        stored = sem("stored")

        block = ctx.enter_context(nc.Block())

        @block.sync
        def _(sp):
            def copy_k(head, n, nqk):
                cols = slice(n * HALF, (n + 1) * HALF)
                sp.wait_ge(qk_low, nqk + 1)
                for kk in (k_hh[head % 2], k_ll[head % 2]):
                    kk = kk[:, cols].bitcast(f32)
                    sp.dma_start(kk[0:D], kk[D:P]).then_inc(qk_copied, 16)

            sp.sem_inc(stored, 16)
            for c in range(RING):
                sp.dma_start(ring[c][:], x_chunk(0, c)).then_inc(ring_loaded[c], 16)
            sp.dma_start(w_stage[:, 0, 0:3 * C], w_qkv[0:P, :]).then_inc(w_loaded[0], 16)
            sp.dma_start(w_stage[:, 1, 0:3 * C], w_qkv[P:2 * P, :]).then_inc(w_loaded[1], 16)
            sp.dma_start(idm[:], ident).then_inc(const_loaded, 16)
            bq = b_qkv.rearrange("(h c) -> c h", c=3 * D)
            sp.dma_start(bqk[:], bq[0:P, :], allow_slow_non_contiguous=True).then_inc(const_loaded, 16)
            bvv = b_qkv.rearrange("(k a c) -> a c k", a=2, c=3 * D)
            for a in range(2):
                sp.dma_start(bv[a * D:(a + 1) * D, :], bvv[a, 2 * D:3 * D, :],
                             allow_slow_non_contiguous=True).then_inc(const_loaded, 16)
            sp.dma_start(bp[:], b_proj.rearrange("(m c) -> c m", c=P),
                         allow_slow_non_contiguous=True).then_inc(const_loaded, 16)
            for c in range(RING, X_CHUNKS):
                sp.wait_ge(x_low, c - RING + 1)
                sp.dma_start(ring[c % RING][:], x_chunk(0, c)).then_inc(ring_loaded[c % RING], 16)
            for k in range(2, KT):
                sp.wait_ge(w_low, 3 * (k - 1))
                sp.dma_start(w_stage[:, k % 2, 0:3 * C],
                             w_qkv[k * P:(k + 1) * P, :]).then_inc(w_loaded[k % 2], 16)
            for k in range(0, KT, 2):
                sp.wait_ge(w_low, 3 * KT if k else 3 * (KT - 1))
                sp.dma_start(w_stage[:, k // 2, 0:2 * C].rearrange("p (k n) -> p k n", k=2),
                             w_proj[k * P:(k + 2) * P, :].rearrange("(k p) n -> p k n", p=P)
                             ).then_inc(w_loaded[k // 2], 16)
            for head in range(2):
                for n in range(NH):
                    copy_k(head, n, 2 * head + n)

            def body(b, more):
                nqk = QKS * b + QK0
                step = 0
                loads = list(LOADS0)
                for h in range(HEADS):
                    for t in range(IT):
                        kind, head, n, ahead, part, parts = PROJECT.get((h, t), NOTHING)
                        if kind == "qk" and part == parts - 1 and (more or not ahead):
                            copy_k(head, n, nqk + step)
                            step += 1
                        if more and (h, t) in X_LOAD:
                            if (h, t) == (1, 3):
                                sp.wait_ge(stored, 16 * OUTS * b + 16)
                            for c in X_LOAD[h, t]:
                                if c >= RING:
                                    sp.wait_ge(x_low, X_CHUNKS * b + (X_CHUNKS + c - RING + 1))
                                sp.dma_start(ring[c % RING][:], x_chunk(b + 1, c)
                                             ).then_inc(ring_loaded[c % RING], 16)
                if more:
                    sp.wait_ge(x_low, X_CHUNKS * b + 2 * X_CHUNKS)
                else:
                    sp.wait_ge(stored, 16 * OUTS * b + 16)
                for g in range(RING):
                    i = (X_CHUNKS + g) % RING
                    sp.dma_start(ring[i][:], tile_of(x, b, g)).then_inc(ring_loaded[i], 16)
                if more:
                    for n in range(NH):
                        copy_k(1, n, nqk + step)
                        step += 1
                for g in range(OUTS):
                    i = (X_CHUNKS + g) % RING
                    sp.wait_ge(out_done, OUTS * b + (g + 2))
                    sp.dma_start(tile_of(out, b, g), ring[i][:]).then_inc(stored, 16)
                    if g + RING < OUTS:
                        sp.wait_ge(stored, 16 * OUTS * b + 16 * (g + 2))
                        sp.dma_start(ring[i][:], tile_of(x, b, g + RING)).then_inc(ring_loaded[i], 16)

            with sp.Fori(0, BATCH - 1) as b:
                body(b, True)
            body(BATCH - 1, False)
            sp.wait_ge(stored, 16 * OUTS * BATCH + 16)

        @block.tensor
        def _(pe):
            def product(bank, w, w_col, r, r_col, part, parts):
                terms = [(k, i, j) for k in range(KT) for i, j in ((0, 0), (0, 1), (1, 0))]
                each = len(terms) // parts
                for e in range(part * each, (part + 1) * each):
                    k, i, j = terms[e]
                    last = nc.tensor.matmul(bank[:], w_col(w[i], k), r_col(r[j], k),
                                            start=e == 0, stop=e == len(terms) - 1)
                return last

            def project_qk(bank, head, n, part=0, parts=1):
                return product(bank, wqk, lambda w, k: w[:, k, head, :],
                               xs, lambda a, k: a[:, k, n * HALF:(n + 1) * HALF], part, parts)

            def project_v(bank, pair, n, part=0, parts=1):
                return product(bank, wv, lambda w, k: w[:, k, 2 * pair:2 * pair + 2, :],
                               xs, lambda a, k: a[:, k, n * HALF:(n + 1) * HALF], part, parts)

            def project_out(bank, g):
                n, m = g // KT, g % KT
                return product(bank, wp, lambda w, k: w[:, k, m * P:(m + 1) * P],
                               os_, lambda a, k: a[:, k, n * HALF:(n + 1) * HALF], 0, 1)

            def score(u):
                head, it = u // IT, u % IT
                i = head % 2
                for n in range(NH):
                    for e, kk in enumerate((k_hh, k_ll)):
                        last = nc.tensor.matmul(scores[u % 2][:, n * HALF:(n + 1) * HALF],
                                                q_hl[i][:, it * P:(it + 1) * P],
                                                kk[i][:, n * HALF:(n + 1) * HALF],
                                                start=e == 0, stop=e == 1)
                return last

            def turn(bank, blocks):
                for j, blk in enumerate(blocks):
                    last = nc.tensor.transpose(turned[bank][:, j, :], blk, idm[:])
                return last

            pe.wait_ge(w_low, 3 * KT)
            for i in range(4):
                pe.wait_ge(x_low, KT * (i % 2 + 1))
                if i > 0:
                    pe.wait_ge(qk_low, i)
                project_qk(ps_g, i // 2, i % 2).then_inc(group_done, 1)
            pe.wait_ge(const_loaded, 16 * 5)
            for n in range(NH):
                if n == 0:
                    pe.wait_ge(qk_low, QK0)
                else:
                    pe.wait_ge(vt_done, n)
                project_v(ps_g, 0, n).then_inc(group_done, 1)
                if n == 0:
                    pe.wait_ge(vt_done, n + 1)
                    turn(0, [v_t[:, j * P:(j + 1) * P] for j in range(QT)]).then_inc(fill_done, 1)
            pe.wait_ge(qk_copied, COPIED * QK0)
            for u in range(2):
                score(u).then_inc(scores_done, 1)

            def body(b, more):
                fill, nqk, nv = FILLS0, QK0, V0
                last_g = "out"

                def g_free():
                    if last_g == "qk":
                        pe.wait_ge(qk_low, QKS * b + nqk)
                    elif last_g == "v":
                        pe.wait_ge(vt_done, VS * b + nv)
                    else:
                        pe.wait_ge(out_done, OUTS * b + 1)
                        pe.wait_ge(qk_low, QKS * b + nqk)
                        pe.wait_ge(vt_done, VS * b + nv)

                def attend(q, part, fills):
                    head, quarter = q // (IT // 2), q % (IT // 2)
                    cols = slice((quarter % 2) * QUARTER, (quarter % 2 + 1) * QUARTER)
                    if part == 0:
                        pe.wait_ge(fill_low, FILLS * b + fills)
                        if q == 0:
                            pe.wait_ge(out_done, OUTS * b + 1)
                        elif q % 2 == 0:
                            pe.wait_ge(o_done, 2 * HEADS * b + q // 2)
                    for jt in range(QT * part, QT * (part + 1)):
                        for e in range(2):
                            last = nc.tensor.matmul(ps_o[:, cols], v_hl[head // 2 % 2][:, jt, head % 2, :],
                                                    pt[e][:, q % 2, jt, :],
                                                    start=jt == 0 and e == 0, stop=jt == IT - 1 and e == 1)
                    if part:
                        last.then_inc(pv_done, 1)

                for h in range(HEADS):
                    for t in range(IT):
                        u = h * IT + t
                        before = fill
                        if more or u + 2 < UNITS:
                            nxt = (u + 2) % UNITS
                            pe.wait_ge(exp_done, UNITS * b + (u + 1))
                            if nxt % IT == 0:
                                pe.wait_ge(qk_copied, COPIED * QKS * b + COPIED * nqk)
                            score(nxt).then_inc(scores_done, 1)
                        pe.wait_ge(norm_done, UNITS * b + (u + 1))
                        for f in range(2):
                            if u == 0:
                                pe.wait_ge(qk_low, QKS * b + QK0)
                            pe.wait_ge(fill_low, FILLS * b + max(fill - 1, 1))
                            turn(fill % 2, [probs[u % 2][:, j * P:(j + 1) * P]
                                            for j in range(QT * f, QT * (f + 1))]).then_inc(fill_done, 1)
                            fill += 1
                        if u >= 2:
                            attend(u // 2 - 1, u % 2, before)
                        if (h, t) in V_TURN and (more or not V_TURN[h, t][2]):
                            pe.wait_ge(fill_low, FILLS * b + (fill - 1))
                            pe.wait_ge(vt_done, VS * b + nv)
                            turn(fill % 2, [v_t[:, j * P:(j + 1) * P] for j in range(QT)]
                                 ).then_inc(fill_done, 1)
                            fill += 1
                        kind, head, n, ahead, part, parts = PROJECT.get((h, t), NOTHING)
                        if kind and (more or not ahead):
                            if part == 0:
                                g_free()
                            if kind == "qk":
                                if ahead and part == 0:
                                    pe.wait_ge(x_low, X_CHUNKS * b + (X_CHUNKS + KT * (n + 1)))
                                last = project_qk(ps_g, head, n, part, parts)
                            else:
                                last = project_v(ps_g, head, n, part, parts)
                            if part == parts - 1:
                                last.then_inc(group_done, 1)
                                nqk += kind == "qk"
                                nv += kind == "v"
                                last_g = kind
                for part in range(2):
                    attend(PVS - 1, part, fill)
                if more:
                    g_free()
                    project_qk(ps_g, 1, 0).then_inc(group_done, 1)
                    project_qk(turned_flat, 1, 1).then_inc(group_done, 1)
                    nqk += NH
                    last_g = "qk"
                if not more:
                    pe.wait_ge(w_low, 3 * KT + 2)
                for g in range(OUTS):
                    n = g // KT
                    if g % KT == 0:
                        pe.wait_ge(os_low, 2 * KT * b + KT * (n + 1))
                    if g == 0:
                        pe.wait_ge(o_done, 2 * HEADS * b + 2 * HEADS)
                        pe.wait_ge(w_low, 3 * KT + 2)
                    elif g == 1:
                        if more:
                            pe.wait_ge(qk_low, QKS * b + (nqk - 1))
                        else:
                            g_free()
                    else:
                        pe.wait_ge(out_done, OUTS * b + g)
                    project_out(ps_o if g % 2 == 0 else ps_g, g).then_inc(group_done, 1)

            with pe.Fori(0, BATCH - 1) as b:
                body(b, True)
            body(BATCH - 1, False)

        @block.scalar
        def _(act):
            def exponentials(u, unit):
                act.wait_ge(max_done, unit + 1)
                nc.scalar.activation(probs[u % 2][:], scores[u % 2][:], ACT.Exp, bias=negmax[:, u % 2:u % 2 + 1],
                                     scale=1.0, accum_out=sums[:, u % 2:u % 2 + 1]).then_inc(exp_done, 1)

            def qk_high_part(head, n, bank):
                cols = slice(n * HALF, (n + 1) * HALF)
                for dst, rows in ((q_hl, slice(0, D)), (k_hh, slice(D, P))):
                    nc.scalar.activation(dst[head % 2][rows, cols], bank[rows, :], ACT.Identity,
                                         bias=bqk[rows, head:head + 1], scale=1.0).then_inc(qk_high, 1)

            def stage_v(pair):
                nc.scalar.activation(v_t[:], ps_g[:], ACT.Identity,
                                     bias=bv[:, pair:pair + 1], scale=1.0).then_inc(vt_done, 1)

            def split_x(c, slot):
                k, n = c % KT, c // KT
                nc.scalar.activation(xs[0][:, k, n * HALF:(n + 1) * HALF], ring[slot][:],
                                     ACT.Copy).then_inc(x_high, 1)

            def v_high(pair, n, bank):
                nc.scalar.activation(v_hl[pair % 2][:, QT * n:QT * (n + 1), :, 0:D],
                                     turned[bank][:].rearrange("p j (a d) -> p j a d", a=2),
                                     ACT.Copy).then_inc(fill_high, 1)

            for c in range(RING):
                act.wait_ge(ring_loaded[c], 16)
                split_x(c, c)
            for k in range(KT):
                act.wait_ge(w_loaded[k % 2], 16 * (k // 2 + 1))
                for part, (dst, scale) in enumerate(((wqk[0][:, k, :, 0:D], SCALE), (wqk[0][:, k, :, D:P], 1.0),
                                                     (wv[0][:, k, :, :], 1.0))):
                    src = w_stage[:, k % 2, 0:3 * C].rearrange("p (h c) -> p h c", h=HEADS)
                    nc.scalar.activation(dst, src[:, :, part * D:(part + 1) * D], ACT.Copy,
                                         scale=scale).then_inc(w_high, 1)
                if k < 2:
                    for c in range(RING + 3 * k, min(RING + 3 * k + 3, X_CHUNKS)):
                        act.wait_ge(ring_loaded[c % RING], 16 * (c // RING + 1))
                        split_x(c, c % RING)
            act.wait_ge(b_scaled, 1)
            for i in range(QK0):
                act.wait_ge(group_done, i + 1)
                qk_high_part(i // 2, i % 2, ps_g)
            for n in range(NH):
                act.wait_ge(group_done, QK0 + n + 1)
                if n:
                    act.wait_ge(fill_done, n)
                stage_v(0)
                if n == 0:
                    act.wait_ge(fill_done, 1)
                    v_high(0, 0, 0)
            for i in range(2):
                act.wait_ge(w_loaded[i], 16 * 3)
                nc.scalar.activation(wp[0][:, 2 * i:2 * i + 2, :],
                                     w_stage[:, i, 0:2 * C].rearrange("p (k n) -> p k n", k=2),
                                     ACT.Copy).then_inc(w_high, 1)
            for u in range(2):
                exponentials(u, u)

            def body(b, more):
                fill, group = FILLS0, GROUPS0
                loads = list(LOADS0)

                def lower_half_out(half_index):
                    act.wait_ge(pv_done, PVS * b + 2 * (half_index + 1))
                    if half_index:
                        act.wait_ge(o_done, 2 * HEADS * b + half_index)
                    nc.scalar.copy(o_low[:], ps_o[D:P, :]).then_inc(olow_done, 1)

                for h in range(HEADS):
                    for t in range(IT):
                        u = h * IT + t
                        for f in range(2):
                            act.wait_ge(fill_done, FILLS * b + (fill + 1))
                            if u == 0 and f == 0:
                                act.wait_ge(group_done, GROUPS * b + GROUPS0)
                            elif u % 2 == 0 and u >= 4 and f == 0:
                                act.wait_ge(pv_done, PVS * b + (u // 2 - 1))
                            col = (u % 2) * P
                            nc.scalar.activation(pt[0][:, u // 2 % 2, QT * f:QT * (f + 1), col:col + P],
                                                 turned[fill % 2][:],
                                                 ACT.Copy).then_inc(fill_high, 1)
                            fill += 1
                        if more or u + 2 < UNITS:
                            exponentials(u, UNITS * b + (u + 2))
                        kind, head, n, ahead, part, parts = PROJECT.get((h, t), NOTHING)
                        if u % 4 == 1 and u >= 5:
                            lower_half_out((u - 5) // 4)
                        if (h, t) in V_TURN and (more or not V_TURN[h, t][2]):
                            act.wait_ge(fill_done, FILLS * b + (fill + 1))
                            v_high(V_TURN[h, t][0], V_TURN[h, t][1], fill % 2)
                            fill += 1
                        if kind and part == parts - 1 and (more or not ahead):
                            group += 1
                            act.wait_ge(group_done, GROUPS * b + group)
                            if kind == "qk":
                                qk_high_part(head, n, ps_g)
                            else:
                                act.wait_ge(fill_done, FILLS * b + fill)
                                stage_v(head)
                        for c in X_SPLIT.get((h, t), ()) if more else ():
                            slot = c % RING
                            loads[slot] += 1
                            act.wait_ge(ring_loaded[slot], 16 * LOADS[slot] * b + 16 * loads[slot])
                            split_x(c, slot)
                lower_half_out(2 * HEADS - 1)
                for n in range(NH):
                    for k in range(KT):
                        if k == 2 and more:
                            group += 1
                            act.wait_ge(group_done, GROUPS * b + group)
                            qk_high_part(1, n, ps_g if n == 0 else turned_flat)
                        if k == KT - 1 and n == 0:
                            act.wait_ge(o_done, 2 * HEADS * b + 2 * HEADS)
                        nc.scalar.activation(os_[0][:, k, n * HALF:(n + 1) * HALF], o[:, k, n * HALF:(n + 1) * HALF],
                                             ACT.Copy).then_inc(os_high, 1)

            with act.Fori(0, BATCH - 1) as b:
                body(b, True)
            body(BATCH - 1, False)

        @block.vector
        def _(dve):
            def maximum(u, unit):
                dve.wait_ge(scores_done, unit + 1)
                nc.vector.tensor_reduce(negmax[:, u % 2:u % 2 + 1], scores[u % 2][:], AXX, ALU.max,
                                        negate=True).then_inc(max_done, 1)

            def reciprocal(u, unit):
                dve.wait_ge(exp_done, unit + 1)
                nc.vector.reciprocal(rinv[:, u % 2:u % 2 + 1], sums[:, u % 2:u % 2 + 1]).then_inc(recip_done, 1)

            def qk_low_part(head, n, bank, high_parts):
                i, cols = head % 2, slice(n * HALF, (n + 1) * HALF)
                for e, (dst, to, high, rows) in enumerate(((q_hl[i], slice(D, P), q_hl[i], slice(0, D)),
                                                           (k_ll[i], slice(D, P), k_hh[i], slice(D, P)))):
                    dve.wait_ge(qk_high, high_parts + (e + 1))
                    last = nc.vector.scalar_tensor_tensor(out=dst[to, cols], in0=bank[rows, :],
                                                          scalar=bqk[rows, head:head + 1],
                                                          in1=high[rows, cols].bitcast(f32),
                                                          op0=ALU.add, op1=ALU.subtract)
                last.then_inc(qk_low, 1)

            def v_low(pair, n, bank):
                v = v_hl[pair % 2][:, QT * n:QT * (n + 1), :, :]
                nc.vector.tensor_tensor(v[:, :, :, D:P], turned[bank][:].rearrange("p j (a d) -> p j a d", a=2),
                                        v[:, :, :, 0:D].bitcast(f32), ALU.subtract).then_inc(fill_low, 1)

            dve.wait_ge(const_loaded, 16 * 5)
            nc.vector.tensor_scalar(bqk[0:D, :], bqk[0:D, :], SCALE, None, ALU.mult).then_inc(b_scaled, 1)
            nc.vector.memset(rinv[:], 0.0).then_inc(out_done, 1)
            for k in range(KT):
                src = w_stage[:, k % 2, 0:3 * C].rearrange("p (h c) -> p h c", h=HEADS)
                for part, (hi, lo, scale) in enumerate(
                        ((wqk[0][:, k, :, 0:D], wqk[1][:, k, :, 0:D], SCALE),
                         (wqk[0][:, k, :, D:P], wqk[1][:, k, :, D:P], 1.0),
                         (wv[0][:, k, :, :], wv[1][:, k, :, :], 1.0))):
                    dve.wait_ge(w_high, 3 * k + part + 1)
                    nc.vector.scalar_tensor_tensor(out=lo, in0=src[:, :, part * D:(part + 1) * D], scalar=scale,
                                                   in1=hi.bitcast(f32), op0=ALU.mult,
                                                   op1=ALU.subtract).then_inc(w_low, 1)
            dve.wait_ge(b_scaled, 1)
            for i in range(QK0):
                qk_low_part(i // 2, i % 2, ps_g, 2 * i)
            dve.wait_ge(fill_high, 1)
            v_low(0, 0, 0)
            for i in range(2):
                dve.wait_ge(w_high, 3 * KT + i + 1)
                nc.vector.tensor_tensor(wp[1][:, 2 * i:2 * i + 2, :],
                                        w_stage[:, i, 0:2 * C].rearrange("p (k n) -> p k n", k=2),
                                        wp[0][:, 2 * i:2 * i + 2, :].bitcast(f32),
                                        ALU.subtract).then_inc(w_low, 1)
            for u in range(2):
                maximum(u, u)
            for u in range(2):
                reciprocal(u, u)

            def body(b, more):
                fill, nqk = FILLS0, QK0
                loads = list(LOADS0)

                def whole_out(half_index):
                    head, half = half_index // 2, half_index % 2
                    rows = slice((head % 2) * D, (head % 2 + 1) * D)
                    dve.wait_ge(olow_done, 2 * HEADS * b + (half_index + 1))
                    nc.vector.tensor_tensor(o[rows, head // 2, half * HALF:(half + 1) * HALF], ps_o[0:D, :],
                                            o_low[:], ALU.add).then_inc(o_done, 1)

                for h in range(HEADS):
                    for t in range(IT):
                        u = h * IT + t
                        ahead_unit = more or u + 2 < UNITS
                        if ahead_unit:
                            maximum(u, UNITS * b + (u + 2))
                        for f in range(2):
                            dve.wait_ge(fill_high, FILLS * b + (fill + 1))
                            part = (slice(None), u // 2 % 2, slice(QT * f, QT * (f + 1)),
                                    slice((u % 2) * P, (u % 2 + 1) * P))
                            nc.vector.tensor_tensor(pt[1][part], turned[fill % 2][:], pt[0][part].bitcast(f32),
                                                    ALU.subtract).then_inc(fill_low, 1)
                            fill += 1
                        if ahead_unit:
                            reciprocal(u, UNITS * b + (u + 2))
                        kind, head, n, ahead, part, parts = PROJECT.get((h, t), NOTHING)
                        if u % 4 == 1 and u >= 5:
                            whole_out((u - 5) // 4)
                        if (h, t) in V_TURN and (more or not V_TURN[h, t][2]):
                            dve.wait_ge(fill_high, FILLS * b + (fill + 1))
                            v_low(V_TURN[h, t][0], V_TURN[h, t][1], fill % 2)
                            fill += 1
                        if kind == "qk" and part == parts - 1 and (more or not ahead):
                            qk_low_part(head, n, ps_g, 2 * QKS * b + 2 * nqk)
                            nqk += 1
                        for c in X_SPLIT.get((h, t), ()) if more else ():
                            loads[c % RING] += 1
                whole_out(2 * HEADS - 1)
                for n in range(NH):
                    for k in range(KT):
                        if k == 2 and more:
                            qk_low_part(1, n, ps_g if n == 0 else turned_flat, 2 * QKS * b + 2 * nqk)
                            nqk += 1
                        dve.wait_ge(os_high, 2 * KT * b + (KT * n + k + 1))
                        src = o[:, k, n * HALF:(n + 1) * HALF]
                        if k == KT - 1 and n == 0:
                            dve.wait_ge(o_done, 2 * HEADS * b + 2 * HEADS)
                        nc.vector.tensor_tensor(os_[1][:, k, n * HALF:(n + 1) * HALF], src,
                                                os_[0][:, k, n * HALF:(n + 1) * HALF].bitcast(f32),
                                                ALU.subtract).then_inc(os_low, 1)
                for g in range(OUTS):
                    slot = (X_CHUNKS + g) % RING
                    loads[slot] += 1
                    group = GROUPS0 + (GROUPS - OUTS) - (0 if more else 6) + g + 1
                    dve.wait_ge(group_done, GROUPS * b + group)
                    dve.wait_ge(ring_loaded[slot], 16 * LOADS[slot] * b + 16 * loads[slot])
                    nc.vector.scalar_tensor_tensor(out=ring[slot][:], in0=(ps_o if g % 2 == 0 else ps_g)[:],
                                                   scalar=bp[:, g % KT:g % KT + 1], in1=ring[slot][:],
                                                   op0=ALU.add, op1=ALU.add).then_inc(out_done, 1)

            with dve.Fori(0, BATCH - 1) as b:
                body(b, True)
            body(BATCH - 1, False)

        @block.gpsimd
        def _(pool):
            def split_x(c, slot):
                k, n = c % KT, c // KT
                cols = slice(n * HALF, (n + 1) * HALF)
                nc.gpsimd.tensor_tensor(xs[1][:, k, cols], ring[slot][:], xs[0][:, k, cols].bitcast(f32),
                                        ALU.subtract).then_inc(x_low, 1)

            def normalise(u, unit):
                pool.wait_ge(recip_done, unit + 1)
                nc.gpsimd.tensor_tensor(probs[u % 2][:], probs[u % 2][:],
                                        rinv[:, u % 2:u % 2 + 1].broadcast_to([P, S]),
                                        ALU.mult).then_inc(norm_done, 1)

            for c in range(X_CHUNKS):
                pool.wait_ge(x_high, c + 1)
                split_x(c, c % RING)
            for u in range(2):
                normalise(u, u)

            def body(b, more):
                for h in range(HEADS):
                    for t in range(IT):
                        u = h * IT + t
                        if more or u + 2 < UNITS:
                            normalise(u, UNITS * b + (u + 2))
                        for c in X_SPLIT.get((h, t), ()) if more else ():
                            pool.wait_ge(x_high, X_CHUNKS * b + (X_CHUNKS + c + 1))
                            split_x(c, c % RING)

            with pool.Fori(0, BATCH - 1) as b:
                body(b, True)
            body(BATCH - 1, False)


def kernel(x, L0_conv_w_qkv, L0_conv_b_qkv, L0_conv_w_proj, L0_conv_b_proj):
    import numpy as np
    import concourse.bacc as bacc
    from concourse.bass_utils import run_bass_kernel_spmd

    x = np.asarray(x)
    batch, channels, height, width = x.shape
    arrays = {
        "x_in": np.ascontiguousarray(x).reshape(batch, channels, height * width),
        "w_qkv_in": np.ascontiguousarray(L0_conv_w_qkv),
        "b_qkv_in": np.ascontiguousarray(L0_conv_b_qkv),
        "w_proj_in": np.ascontiguousarray(L0_conv_w_proj),
        "b_proj_in": np.ascontiguousarray(L0_conv_b_proj),
        "ident_in": np.eye(128, dtype=np.float32),
    }
    nc = bacc.Bacc("TRN2", target_bir_lowering=False, num_devices=1)
    ins = [nc.dram_tensor(n, a.shape, mybir.dt.from_np(a.dtype), kind="ExternalInput").ap()
           for n, a in arrays.items()]
    out = nc.dram_tensor("out", arrays["x_in"].shape, mybir.dt.float32, kind="ExternalOutput").ap()
    attention_kernel(nc, *ins, out)
    result = run_bass_kernel_spmd(nc, [arrays], core_ids=[0])
    return result.results[0]["out"].reshape(x.shape)
```

```python
import concourse.bass as bass
from concourse import mybir
from contextlib import ExitStack


def attention_kernel(nc, x, w_qkv, b_qkv, w_proj, b_proj, ident, out):
    f32, f32r = mybir.dt.float32, mybir.dt.float32r
    ACT = mybir.ActivationFunctionType
    ALU = mybir.AluOpType
    AXX = mybir.AxisListType.X

    P = 128
    BATCH, C, S = x.shape
    HEADS = 8
    D = C // HEADS
    SCALE = float(D) ** -0.5
    KT = C // P
    NH = 2
    HALF = S // NH
    PAIRS = HEADS // 2
    IT = S // P
    UNITS = HEADS * IT
    QT = IT // NH
    QUARTER = 2 * P
    PVS = UNITS // 2

    TERMS = [(k, i, j) for k in range(KT) for i, j in ((0, 0), (0, 1), (1, 0))]
    KT_TERMS = len(TERMS) // KT
    PROJECT = {}

    def place(start, shares, *group):
        assert sum(shares) == len(TERMS)
        each = 2 if group[0] == "v" else 1
        for e, share in enumerate(shares):
            u = start[0] * IT + start[1] + e
            if share:
                PROJECT[u // IT, u % IT] = (*group, each * sum(shares[:e]), each * sum(shares[:e + 1]),
                                            e == len(shares) - 1)

    place((0, 0), [3, 3, 3, 3], "qk", 1, 1, False)
    place((0, 4), [4, 4, 4], "qk", 2, 0, False)
    place((0, 7), [4, 4, 4], "qk", 2, 1, False)
    place((1, 4), [4, 4, 4], "qk", 3, 0, False)
    place((1, 7), [4, 4, 4], "qk", 3, 1, False)
    place((2, 2), [6, 6], "v", 1, 0, False)
    place((2, 4), [6, 6], "v", 1, 1, False)
    place((2, 6), [6, 6], "qk", 4, 0, False)
    place((3, 0), [4, 4, 4], "qk", 4, 1, False)
    place((3, 3), [4, 4, 4], "v", 1, 2, False)
    place((3, 6), [6, 6], "v", 1, 3, False)
    place((4, 0), [6, 6], "qk", 5, 0, False)
    place((4, 2), [6, 6], "qk", 5, 1, False)
    place((4, 4), [3, 3, 3, 3], "qk", 6, 0, False)
    place((5, 0), [3, 3, 3, 3], "qk", 6, 1, False)
    place((5, 4), [4, 4, 4], "qk", 7, 0, False)
    place((5, 7), [3, 3, 3, 3], "qk", 7, 1, False)
    place((6, 3), [4, 4, 4], "qk", 0, 0, True)
    place((6, 6), [6, 6], "v", 0, 0, True)
    place((7, 0), [6, 6], "v", 0, 1, True)
    place((7, 2), [6, 6], "qk", 0, 1, True)
    place((7, 4), [6, 6], "v", 0, 2, True)
    place((7, 6), [6, 6], "v", 0, 3, True)
    X_CHUNKS = KT * NH
    RING = 3
    X_SPLIT = {divmod(5 * IT + 7 + c, IT): (c,) for c in range(X_CHUNKS)}
    X_LOAD = {slot: (cs[0] + RING,) for slot, cs in X_SPLIT.items() if cs[0] + RING < X_CHUNKS}
    X_LOAD[1, 3] = range(RING)
    V_PLACE = (1, 2, 1, 0)
    V_HEADS = [0, 1, 2, 3, 6, 7, 4, 5]
    NOTHING = ("", 0, 0, False, 0, 0, False)

    GROUPS0, GROUPS = 7, 32
    QK0, QKS = 3, 2 * HEADS
    V0, VS = 4, 2 * PAIRS
    FILLS = 2 * UNITS
    OUTS = KT * NH
    W_PARTS = 5
    COPIED = NH * 2 * 16
    LOADS0 = [2, 2, 1]
    LOADS = [sum(c % RING == i for c in range(X_CHUNKS)) for i in range(RING)]

    def x_chunk(b, c):
        k, n = c % KT, c // KT
        return x[b, k * P:(k + 1) * P, n * HALF:(n + 1) * HALF]

    def tile_of(t, b, g):
        n, m = g // KT, g % KT
        return t[b, m * P:(m + 1) * P, n * HALF:(n + 1) * HALF]

    ctx = ExitStack()
    with ctx:
        def sb(name, shape, dt=f32):
            return ctx.enter_context(nc.sbuf_tensor(name, shape, dt))

        def sem(name):
            return ctx.enter_context(nc.semaphore(name))

        wqk = [sb(f"wqk_{s}", [P, KT, HEADS, P], f32r) for s in "hl"]
        wv = [sb(f"wv_{s}", [P, KT, HEADS, D], f32r) for s in "hl"]
        wp = [sb(f"wp_{s}", [P, KT, C], f32r) for s in "hl"]
        xs = [sb(f"x_{s}", [P, KT, S], f32r) for s in "hl"]
        q_hl = [sb(f"q_hl{i}", [P, S], f32r) for i in range(2)]
        k_hh = [sb(f"k_hh{i}", [P, S], f32r) for i in range(2)]
        k_ll = [sb(f"k_ll{i}", [P, S], f32r) for i in range(2)]
        v_hl = sb("v_hl", [P, IT, 6, P], f32r)
        pt = [sb(f"pt_{s}", [P, 2, IT, QUARTER], f32r) for s in "hl"]
        os_ = [t[:].rearrange("p i a b -> p (i a b)").rearrange("p (k s) -> p k s", k=KT) for t in pt]
        probs_both = sb("probs", [P, 2, S])
        probs = [probs_both[:, i, :] for i in range(2)]
        o = sb("o", [P, PAIRS, S])
        ring = [sb(f"ring{i}", [P, HALF]) for i in range(RING)]
        idm = sb("idm", [P, P])
        bqk = sb("bqk", [P, HEADS])
        bv = sb("bv", [P, PAIRS])
        bp = sb("bp", [P, KT])
        negmax = sb("negmax", [P, 2])
        sums = sb("sums", [P, 2])
        rinv = sb("rinv", [P, 2])
        W = 3 * C
        o_flat = o[:].rearrange("p a b -> p (a b)")
        probs_flat = probs_both[:].rearrange("p i s -> p (i s)")
        w_stage = [m[:, at:at + W].rearrange("p (h c) -> p h c", h=HEADS)
                   for m, at in ((o_flat, 0), (o_flat, W), (probs_flat, 0), (o_flat, 0))]
        wp_stage = o_flat[:, W:W + KT * C].rearrange("p (k n) -> p k n", k=KT)
        x_stage = [(ring[c][:], 1) for c in range(RING)] + [(ring[0][:], 2)] + [
            (m[:, at:at + HALF], 1) for m, at in ((o_flat, 2 * W), (o_flat, 2 * W + HALF), (probs_flat, W))
        ] + [(ring[1][:], 2)]
        X_FIRST = [k + n * KT for k in range(KT) for n in range(NH)]

        scores = [ctx.enter_context(nc.psum_tensor(f"scores{i}", [P, S], f32)) for i in range(2)]
        turned = [ctx.enter_context(nc.psum_tensor(f"turned{i}", [P, 4, P], f32)) for i in range(2)]
        turned_flat = [t[:].rearrange("p j c -> p (j c)") for t in turned]
        ps_o = ctx.enter_context(nc.psum_tensor("ps_o", [P, HALF], f32))
        ps_g = ctx.enter_context(nc.psum_tensor("ps_g", [P, HALF], f32))

        halves = [scores[i][:, n * HALF:(n + 1) * HALF] for i in range(2) for n in range(NH)]

        const_loaded = sem("const_loaded")
        w_loaded = [sem(f"w_loaded{i}") for i in range(KT)]
        wp_loaded = sem("wp_loaded")
        w_high = sem("w_high")
        w_low = sem("w_low")
        b_scaled = sem("b_scaled")
        ring_loaded = [sem(f"ring_loaded{i}") for i in range(RING)]
        x_loaded = [ring_loaded[0], ring_loaded[1], ring_loaded[2], ring_loaded[0]] + [
            sem(f"x_staged{i}") for i in range(3)] + [ring_loaded[1]]
        x_high = sem("x_high")
        x_low = sem("x_low")
        group_done = sem("group_done")
        qk_high = sem("qk_high")
        qk_low = sem("qk_low")
        k_copied = [sem(f"k_copied{i}") for i in range(2)]
        v_high = sem("v_high")
        v_low = sem("v_low")
        scores_done = sem("scores_done")
        max_done = sem("max_done")
        exp_done = sem("exp_done")
        recip_done = sem("recip_done")
        norm_done = sem("norm_done")
        fill_done = sem("fill_done")
        fill_high = sem("fill_high")
        fill_low = sem("fill_low")
        pv_done = sem("pv_done")
        half_moved = sem("half_moved")
        o_done = sem("o_done")
        residual_loaded = [sem(f"residual_loaded{g}") for g in range(OUTS)]
        os_high = sem("os_high")
        os_low = sem("os_low")
        os_low_pool = sem("os_low_pool")
        out_done = sem("out_done")
        stored = sem("stored")

        v_banks = [ps_g[:], ps_o[:]] + turned_flat

        def w_parts(k):
            q = ([t[:, k, :, 0:D] for t in wqk], w_stage[k][:, :, 0:D], SCALE)
            key = ([t[:, k, :, D:P] for t in wqk], w_stage[k][:, :, D:P], 1.0)
            v = [([t[:, k, to:to + count, :] for t in wv],
                  w_stage[k][:, V_HEADS[to]:V_HEADS[to] + count, P:P + D], 1.0)
                 for to, count in ((0, 4), (4, 2), (6, 2))]
            return [q, key] + v

        def v_place(half, pair):
            at = 2 * min(V_PLACE[2 * half:2 * half + 2])
            return v_hl[:, 2 * pair:2 * pair + 2, at:at + 4, :]

        def o_chunk(g):
            return o[:, g % KT, g // KT * HALF:(g // KT + 1) * HALF]

        def o_rows(half_index):
            head, n = half_index // 2, half_index % 2
            at = head % 2 * D
            return o[at:at + D, head // 2, n * HALF:(n + 1) * HALF], slice(D - at, P - at)

        block = ctx.enter_context(nc.Block())

        @block.sync
        def _(sp):
            def copy_k(head, n, nqk):
                cols = slice(n * HALF, (n + 1) * HALF)
                sp.wait_ge(qk_low, nqk + 1)
                for kk in (k_hh[head % 2], k_ll[head % 2]):
                    kk = kk[:, cols].bitcast(f32)
                    sp.dma_start(kk[0:D], kk[D:P]).then_inc(k_copied[head % 2], 16)

            sp.sem_inc(stored, 16)
            for k in range(KT):
                for c in (k, k + KT):
                    dst, loads = x_stage[c]
                    if loads == 2:
                        sp.wait_ge(x_low, X_FIRST.index(0 if c == RING else 1) + 1)
                    sp.dma_start(dst, x_chunk(0, c)).then_inc(x_loaded[c], 16)
                if k == KT - 1:
                    sp.wait_ge(w_low, W_PARTS)
                sp.dma_start(w_stage[k], w_qkv[k * P:(k + 1) * P, :].rearrange("p (h c) -> p h c", h=HEADS)
                             ).then_inc(w_loaded[k], 16)
            bq = b_qkv.rearrange("(h c) -> c h", c=3 * D)
            sp.dma_start(bqk[:], bq[0:P, :], allow_slow_non_contiguous=True).then_inc(const_loaded, 16)
            bvv = b_qkv.rearrange("(k a c) -> a c k", a=2, c=3 * D)
            for a in range(2):
                sp.dma_start(bv[a * D:(a + 1) * D, :], bvv[a, 2 * D:3 * D, :],
                             allow_slow_non_contiguous=True).then_inc(const_loaded, 16)
            sp.dma_start(bp[:], b_proj.rearrange("(m c) -> c m", c=P),
                         allow_slow_non_contiguous=True).then_inc(const_loaded, 16)
            sp.dma_start(idm[:], ident).then_inc(const_loaded, 16)
            sp.wait_ge(w_low, 2 * W_PARTS)
            sp.wait_ge(x_low, X_FIRST.index(KT) + 1)
            sp.dma_start(wp_stage, w_proj.rearrange("(k p) n -> p k n", p=P)).then_inc(wp_loaded, 16)
            for i in range(QK0):
                copy_k(i // NH, i % NH, i)

            def body(b, more):
                nqk = QKS * b + QK0
                step = 0
                for h in range(HEADS):
                    for t in range(IT):
                        kind, head, n, ahead, first, to, done = PROJECT.get((h, t), NOTHING)
                        if kind == "qk" and done and (more or not ahead):
                            copy_k(head, n, nqk + step)
                            step += 1
                        if more and (h, t) in X_LOAD:
                            if (h, t) == (1, 3):
                                sp.wait_ge(x_low, X_CHUNKS * b + X_CHUNKS)
                            for c in X_LOAD[h, t]:
                                if c >= RING:
                                    sp.wait_ge(x_low, X_CHUNKS * b + (X_CHUNKS + c - RING + 1))
                                sp.dma_start(ring[c % RING][:], x_chunk(b + 1, c)
                                             ).then_inc(ring_loaded[c % RING], 16)
                for g in range(OUTS):
                    n, k = divmod(g, KT)
                    if g == KT and more:
                        copy_k(1, 0, nqk + step)
                        step += 1
                    sp.wait_ge((os_low, os_low_pool)[n], KT * b + (k + 1))
                    sp.dma_start(o_chunk(g), tile_of(x, b, g)).then_inc(residual_loaded[g], 16)
                for g in range(OUTS):
                    sp.wait_ge(out_done, OUTS * b + (g + 2))
                    sp.dma_start(tile_of(out, b, g), o_chunk(g)).then_inc(stored, 16)

            with sp.Fori(0, BATCH - 1) as b:
                body(b, True)
            body(BATCH - 1, False)
            sp.wait_ge(stored, 16 * OUTS * BATCH + 16)

        @block.tensor
        def _(pe):
            def product(bank, w, w_col, r, r_col, first, to):
                for e in range(first, to):
                    k, i, j = TERMS[e]
                    last = nc.tensor.matmul(bank, w_col(w[i], k), r_col(r[j], k),
                                            start=e == 0, stop=e == len(TERMS) - 1)
                return last

            def project_qk(bank, head, n, first=0, to=len(TERMS)):
                return product(bank, wqk, lambda w, k: w[:, k, head, :],
                               xs, lambda a, k: a[:, k, n * HALF:(n + 1) * HALF], first, to)

            def project_v(bank, half, pair, first, to):
                for e in range(first, to):
                    tile, term = divmod(e, len(TERMS))
                    k, i, j = TERMS[term]
                    at = (2 * pair + tile) * P
                    last = nc.tensor.matmul(bank[:, tile * 4 * D:(tile + 1) * 4 * D], xs[j][:, k, at:at + P],
                                            wv[i][:, k, 4 * half:4 * half + 4, :],
                                            start=term == 0, stop=term == len(TERMS) - 1)
                return last

            def project_out(bank, g, terms):
                n, m = g // KT, g % KT
                return product(bank, wp, lambda w, k: w[:, k, m * P:(m + 1) * P],
                               os_, lambda a, k: a[:, k, n * HALF:(n + 1) * HALF], *terms)

            def score(u):
                head, it = u // IT, u % IT
                i = head % 2
                for n in range(NH):
                    for e, kk in enumerate((k_hh, k_ll)):
                        last = nc.tensor.matmul(scores[u % 2][:, n * HALF:(n + 1) * HALF],
                                                q_hl[i][:, it * P:(it + 1) * P],
                                                kk[i][:, n * HALF:(n + 1) * HALF],
                                                start=e == 0, stop=e == 1)
                return last

            def turn(bank, blocks):
                for j, blk in enumerate(blocks):
                    last = nc.tensor.transpose(turned[bank][:, j, :], blk, idm[:])
                return last

            for k in range(KT):
                pe.wait_ge(x_low, NH * (k + 1))
                pe.wait_ge(w_low, W_PARTS * (k + 1))
                for i in range(QK0):
                    last = project_qk(halves[i], i // 2, i % 2, k * KT_TERMS, (k + 1) * KT_TERMS)
                    if k == KT - 1:
                        last.then_inc(group_done, 1)
            for i in range(V0):
                if i == 2:
                    pe.wait_ge(k_copied[0], COPIED)
                    pe.wait_ge(qk_low, QK0)
                    for u in range(2):
                        score(u).then_inc(scores_done, 1)
                project_v(v_banks[i], 0, i, 0, 2 * len(TERMS)).then_inc(group_done, 1)
            pe.wait_ge(const_loaded, 16 * 5)

            def body(b, more):
                fill, nqk, nv = 0, QK0, V0
                last_g = "out"

                def g_free():
                    if last_g == "qk":
                        pe.wait_ge(qk_low, QKS * b + nqk)
                    elif last_g == "v":
                        pe.wait_ge(v_low, VS * b + nv)
                    else:
                        pe.wait_ge(out_done, OUTS * b + 1)
                        pe.wait_ge(qk_low, QKS * b + nqk)
                        pe.wait_ge(v_low, VS * b + nv)

                def attend(q, part, fills):
                    head, quarter = q // (IT // 2), q % (IT // 2)
                    cols = slice((quarter % 2) * QUARTER, (quarter % 2 + 1) * QUARTER)
                    if part == 0:
                        pe.wait_ge(fill_low, FILLS * b + fills)
                        if q == 0:
                            pe.wait_ge(out_done, OUTS * b + 1)
                        elif q % 2 == 0:
                            pe.wait_ge(o_done, 2 * HEADS * b + q // 2)
                        if q == PVS // 2:
                            pe.wait_ge(v_low, VS * b + (V0 + VS // 2))
                    for jt in range(QT * part, QT * (part + 1)):
                        for e in range(2):
                            last = nc.tensor.matmul(ps_o[:, cols], v_hl[:, jt, 2 * V_PLACE[head // 2] + head % 2, :],
                                                    pt[e][:, q % 2, jt, :],
                                                    start=jt == 0 and e == 0, stop=jt == IT - 1 and e == 1)
                    if part:
                        last.then_inc(pv_done, 1)

                for h in range(HEADS):
                    for t in range(IT):
                        u = h * IT + t
                        before = fill
                        if more or u + 2 < UNITS:
                            nxt = (u + 2) % UNITS
                            pe.wait_ge(exp_done, UNITS * b + (u + 1))
                            if nxt % IT == 0:
                                pe.wait_ge(k_copied[(h + 1) % 2],
                                           COPIED * (HEADS // 2) * b + COPIED * (1 + (h + 1) // 2))
                            score(nxt).then_inc(scores_done, 1)
                        pe.wait_ge(norm_done, UNITS * b + (u + 1))
                        for f in range(2):
                            if u == 0:
                                pe.wait_ge(qk_low, QKS * b + QK0)
                                pe.wait_ge(v_low, VS * b + V0)
                            else:
                                pe.wait_ge(fill_low, FILLS * b + (fill - 1))
                            turn(fill % 2, [probs[u % 2][:, j * P:(j + 1) * P]
                                            for j in range(QT * f, QT * (f + 1))]).then_inc(fill_done, 1)
                            fill += 1
                        if u >= 2:
                            attend(u // 2 - 1, u % 2, before)
                        kind, which, part, ahead, first, to, done = PROJECT.get((h, t), NOTHING)
                        if kind and (more or not ahead):
                            if first == 0:
                                g_free()
                            if kind == "qk" and ahead:
                                for k in sorted({TERMS[e][0] for e in range(first, to) if e % KT_TERMS == 0}):
                                    pe.wait_ge(x_low, X_CHUNKS * b + (X_CHUNKS + KT * part + k + 1))
                            last = (project_qk if kind == "qk" else project_v)(ps_g[:], which, part, first, to)
                            if done:
                                last.then_inc(group_done, 1)
                                nqk += kind == "qk"
                                nv += kind == "v"
                                last_g = kind
                for part in range(2):
                    attend(PVS - 1, part, fill)
                if more:
                    g_free()
                    project_qk(ps_g[:], 1, 0).then_inc(group_done, 1)
                    nqk += 1
                    last_g = "qk"
                if not more:
                    pe.wait_ge(w_low, W_PARTS * KT + 2)
                for g in range(OUTS):
                    n = g // KT
                    if g == 0:
                        pe.wait_ge(o_done, 2 * HEADS * b + 2 * HEADS)
                        pe.wait_ge(w_low, W_PARTS * KT + 2)
                    elif g == 1:
                        g_free()
                    else:
                        pe.wait_ge(out_done, OUTS * b + g)
                    bank = ps_o if g % 2 == 0 else ps_g
                    if g % KT == 0:
                        each = len(TERMS) // KT
                        for k in range(KT):
                            pe.wait_ge((os_low, os_low_pool)[n], KT * b + (k + 1))
                            last = project_out(bank[:], g, (k * each, (k + 1) * each))
                    else:
                        last = project_out(bank[:], g, (0, len(TERMS)))
                    last.then_inc(group_done, 1)

            with pe.Fori(0, BATCH - 1) as b:
                body(b, True)
            body(BATCH - 1, False)

        @block.scalar
        def _(act):
            def exponentials(u, unit):
                act.wait_ge(max_done, unit + 1)
                nc.scalar.activation(probs[u % 2][:], scores[u % 2][:], ACT.Exp, bias=negmax[:, u % 2:u % 2 + 1],
                                     scale=1.0, accum_out=sums[:, u % 2:u % 2 + 1]).then_inc(exp_done, 1)

            def qk_high_part(head, n, bank):
                cols = slice(n * HALF, (n + 1) * HALF)
                for dst, rows in ((q_hl, slice(0, D)), (k_hh, slice(D, P))):
                    nc.scalar.activation(dst[head % 2][rows, cols], bank[rows, :], ACT.Identity,
                                         bias=bqk[rows, head:head + 1], scale=1.0).then_inc(qk_high, 1)

            def split_x(c, src):
                k, n = c % KT, c // KT
                nc.scalar.activation(xs[0][:, k, n * HALF:(n + 1) * HALF], src,
                                     ACT.Copy).then_inc(x_high, 1)

            def v_high_part(half, pair, bank):
                nc.scalar.activation(v_place(half, pair)[:, :, :, 0:D],
                                     bank.rearrange("p (j a d) -> p j a d", j=2, a=4),
                                     ACT.Copy).then_inc(v_high, 1)

            for k in range(KT):
                for c in (k, k + KT):
                    src, loads = x_stage[c]
                    act.wait_ge(x_loaded[c], 16 * loads)
                    split_x(c, src)
                act.wait_ge(w_loaded[k], 16)
                for dst, src, scale in w_parts(k):
                    nc.scalar.activation(dst[0], src, ACT.Copy, scale=scale).then_inc(w_high, 1)
            act.wait_ge(wp_loaded, 16)
            for i in range(2):
                nc.scalar.activation(wp[0][:, 2 * i:2 * i + 2, :], wp_stage[:, 2 * i:2 * i + 2, :],
                                     ACT.Copy).then_inc(w_high, 1)
            act.wait_ge(b_scaled, 1)
            for i in range(QK0):
                act.wait_ge(group_done, i + 1)
                qk_high_part(i // 2, i % 2, halves[i])
            for i in range(V0):
                if i == 2:
                    for u in range(2):
                        exponentials(u, u)
                act.wait_ge(group_done, QK0 + i + 1)
                v_high_part(0, i, v_banks[i])

            def body(b, more):
                fill, group = 0, GROUPS0
                loads = list(LOADS0)

                def move_half(half_index):
                    act.wait_ge(pv_done, PVS * b + 2 * (half_index + 1))
                    if half_index == 0:
                        act.wait_ge(stored, 16 * OUTS * b + 16)
                    out, other = o_rows(half_index)
                    nc.scalar.copy(out, ps_o[other, :]).then_inc(half_moved, 1)

                for h in range(HEADS):
                    for t in range(IT):
                        u = h * IT + t
                        for f in range(2):
                            act.wait_ge(fill_done, FILLS * b + (fill + 1))
                            if u == 0 and f == 0:
                                act.wait_ge(group_done, GROUPS * b + GROUPS0)
                            elif u % 2 == 0 and u >= 4 and f == 0:
                                act.wait_ge(pv_done, PVS * b + (u // 2 - 1))
                            col = (u % 2) * P
                            nc.scalar.activation(pt[0][:, u // 2 % 2, QT * f:QT * (f + 1), col:col + P],
                                                 turned[fill % 2][:],
                                                 ACT.Copy).then_inc(fill_high, 1)
                            fill += 1
                        if more or u + 2 < UNITS:
                            exponentials(u, UNITS * b + (u + 2))
                        kind, head, n, ahead, first, to, done = PROJECT.get((h, t), NOTHING)
                        if u % 4 == 1 and u >= 5:
                            move_half((u - 5) // 4)
                        if done and (more or not ahead):
                            group += 1
                            act.wait_ge(group_done, GROUPS * b + group)
                            if kind == "qk":
                                qk_high_part(head, n, ps_g)
                            else:
                                v_high_part(head, n, ps_g[:])
                        for c in X_SPLIT.get((h, t), ()) if more else ():
                            slot = c % RING
                            loads[slot] += 1
                            act.wait_ge(ring_loaded[slot], 16 * LOADS[slot] * b + 16 * loads[slot])
                            split_x(c, ring[slot][:])
                move_half(2 * HEADS - 1)
                for n in range(NH):
                    for k in range(KT):
                        if (n, k) == (1, 0) and more:
                            group += 1
                            act.wait_ge(group_done, GROUPS * b + group)
                            qk_high_part(1, 0, ps_g)
                        if k == KT - 1 and n == 0:
                            act.wait_ge(o_done, 2 * HEADS * b + 2 * HEADS)
                        nc.scalar.activation(os_[0][:, k, n * HALF:(n + 1) * HALF], o[:, k, n * HALF:(n + 1) * HALF],
                                             ACT.Copy).then_inc(os_high, 1)

            with act.Fori(0, BATCH - 1) as b:
                body(b, True)
            body(BATCH - 1, False)

        @block.vector
        def _(dve):
            def maximum(u, unit):
                dve.wait_ge(scores_done, unit + 1)
                nc.vector.tensor_reduce(negmax[:, u % 2:u % 2 + 1], scores[u % 2][:], AXX, ALU.max,
                                        negate=True).then_inc(max_done, 1)

            def reciprocal(u, unit):
                dve.wait_ge(exp_done, unit + 1)
                nc.vector.reciprocal(rinv[:, u % 2:u % 2 + 1], sums[:, u % 2:u % 2 + 1]).then_inc(recip_done, 1)

            def qk_low_part(head, n, bank, high_parts):
                i, cols = head % 2, slice(n * HALF, (n + 1) * HALF)
                for e, (dst, to, high, rows) in enumerate(((q_hl[i], slice(D, P), q_hl[i], slice(0, D)),
                                                           (k_ll[i], slice(D, P), k_hh[i], slice(D, P)))):
                    dve.wait_ge(qk_high, high_parts + (e + 1))
                    last = nc.vector.scalar_tensor_tensor(out=dst[to, cols], in0=bank[rows, :],
                                                          scalar=bqk[rows, head:head + 1],
                                                          in1=high[rows, cols].bitcast(f32),
                                                          op0=ALU.add, op1=ALU.subtract)
                last.then_inc(qk_low, 1)

            def v_low_part(half, pair, bank, high_parts):
                v = v_place(half, pair)
                dve.wait_ge(v_high, high_parts + 1)
                nc.vector.tensor_tensor(v[:, :, :, D:P], bank.rearrange("p (j a d) -> p j a d", j=2, a=4),
                                        v[:, :, :, 0:D].bitcast(f32), ALU.subtract).then_inc(v_low, 1)

            nc.vector.memset(rinv[:], 0.0).then_inc(out_done, 1)
            for k in range(KT):
                for part, (dst, src, scale) in enumerate(w_parts(k)):
                    dve.wait_ge(w_high, W_PARTS * k + part + 1)
                    nc.vector.scalar_tensor_tensor(out=dst[1], in0=src, scalar=scale, in1=dst[0].bitcast(f32),
                                                   op0=ALU.mult, op1=ALU.subtract).then_inc(w_low, 1)
            dve.wait_ge(const_loaded, 16 * 5)
            nc.vector.tensor_scalar(bqk[0:D, :], bqk[0:D, :], SCALE, None, ALU.mult).then_inc(b_scaled, 1)
            for i in range(2):
                dve.wait_ge(w_high, W_PARTS * KT + i + 1)
                nc.vector.tensor_tensor(wp[1][:, 2 * i:2 * i + 2, :], wp_stage[:, 2 * i:2 * i + 2, :],
                                        wp[0][:, 2 * i:2 * i + 2, :].bitcast(f32),
                                        ALU.subtract).then_inc(w_low, 1)
            dve.wait_ge(b_scaled, 1)
            for i in range(QK0):
                qk_low_part(i // 2, i % 2, halves[i], 2 * i)
            for i in range(V0):
                if i == 2:
                    for u in range(2):
                        maximum(u, u)
                    for u in range(2):
                        reciprocal(u, u)
                v_low_part(0, i, v_banks[i], i)

            def body(b, more):
                fill, nqk, nv = 0, QK0, V0

                def sum_halves(half_index):
                    out, other = o_rows(half_index)
                    rows = slice(D - other.start, P - other.start)
                    bias = bv[rows, half_index // 4:half_index // 4 + 1]
                    dve.wait_ge(half_moved, 2 * HEADS * b + (half_index + 1))
                    nc.vector.scalar_tensor_tensor(out=out, in0=ps_o[rows, :], scalar=bias, in1=out,
                                                   op0=ALU.add, op1=ALU.add).then_inc(o_done, 1)

                for h in range(HEADS):
                    for t in range(IT):
                        u = h * IT + t
                        ahead_unit = more or u + 2 < UNITS
                        if ahead_unit:
                            maximum(u, UNITS * b + (u + 2))
                        for f in range(2):
                            dve.wait_ge(fill_high, FILLS * b + (fill + 1))
                            part = (slice(None), u // 2 % 2, slice(QT * f, QT * (f + 1)),
                                    slice((u % 2) * P, (u % 2 + 1) * P))
                            nc.vector.tensor_tensor(pt[1][part], turned[fill % 2][:], pt[0][part].bitcast(f32),
                                                    ALU.subtract).then_inc(fill_low, 1)
                            fill += 1
                        if ahead_unit:
                            reciprocal(u, UNITS * b + (u + 2))
                        kind, head, n, ahead, first, to, done = PROJECT.get((h, t), NOTHING)
                        if u % 4 == 1 and u >= 5:
                            sum_halves((u - 5) // 4)
                        if done and (more or not ahead):
                            if kind == "qk":
                                qk_low_part(head, n, ps_g, 2 * QKS * b + 2 * nqk)
                                nqk += 1
                            else:
                                v_low_part(head, n, ps_g[:], VS * b + nv)
                                nv += 1
                sum_halves(2 * HEADS - 1)
                for n in range(NH):
                    for k in range(KT):
                        if (n, k) == (1, 0) and more:
                            qk_low_part(1, 0, ps_g, 2 * QKS * b + 2 * nqk)
                            nqk += 1
                        if n:
                            continue
                        dve.wait_ge(os_high, 2 * KT * b + (k + 1))
                        src = o[:, k, n * HALF:(n + 1) * HALF]
                        if k == KT - 1:
                            dve.wait_ge(o_done, 2 * HEADS * b + 2 * HEADS)
                        nc.vector.tensor_tensor(os_[1][:, k, n * HALF:(n + 1) * HALF], src,
                                                os_[0][:, k, n * HALF:(n + 1) * HALF].bitcast(f32),
                                                ALU.subtract).then_inc(os_low, 1)
                for g in range(OUTS):
                    group = GROUPS0 + (GROUPS - OUTS) - (0 if more else 7) + g + 1
                    dve.wait_ge(group_done, GROUPS * b + group)
                    dve.wait_ge(residual_loaded[g], 16 * b + 16)
                    nc.vector.scalar_tensor_tensor(out=o_chunk(g), in0=(ps_o if g % 2 == 0 else ps_g)[:],
                                                   scalar=bp[:, g % KT:g % KT + 1], in1=o_chunk(g),
                                                   op0=ALU.add, op1=ALU.add).then_inc(out_done, 1)

            with dve.Fori(0, BATCH - 1) as b:
                body(b, True)
            body(BATCH - 1, False)

        @block.gpsimd
        def _(pool):
            def split_x(c, src):
                k, n = c % KT, c // KT
                cols = slice(n * HALF, (n + 1) * HALF)
                nc.gpsimd.tensor_tensor(xs[1][:, k, cols], src, xs[0][:, k, cols].bitcast(f32),
                                        ALU.subtract).then_inc(x_low, 1)

            def normalise(u, unit):
                pool.wait_ge(recip_done, unit + 1)
                nc.gpsimd.tensor_tensor(probs[u % 2][:], probs[u % 2][:],
                                        rinv[:, u % 2:u % 2 + 1].broadcast_to([P, S]),
                                        ALU.mult).then_inc(norm_done, 1)

            for i, c in enumerate(X_FIRST):
                pool.wait_ge(x_high, i + 1)
                split_x(c, x_stage[c][0])
            for u in range(2):
                normalise(u, u)

            def body(b, more):
                for h in range(HEADS):
                    for t in range(IT):
                        u = h * IT + t
                        if more or u + 2 < UNITS:
                            normalise(u, UNITS * b + (u + 2))
                        for c in X_SPLIT.get((h, t), ()) if more else ():
                            pool.wait_ge(x_high, X_CHUNKS * b + (X_CHUNKS + c + 1))
                            split_x(c, ring[c % RING][:])
                for k in range(KT):
                    pool.wait_ge(os_high, 2 * KT * b + (KT + k + 1))
                    nc.gpsimd.tensor_tensor(os_[1][:, k, HALF:S], o[:, k, HALF:S],
                                            os_[0][:, k, HALF:S].bitcast(f32),
                                            ALU.subtract).then_inc(os_low_pool, 1)

            with pool.Fori(0, BATCH - 1) as b:
                body(b, True)
            body(BATCH - 1, False)


def kernel(x, L0_conv_w_qkv, L0_conv_b_qkv, L0_conv_w_proj, L0_conv_b_proj):
    import numpy as np
    import concourse.bacc as bacc
    from concourse.bass_utils import run_bass_kernel_spmd

    x = np.asarray(x)
    batch, channels, height, width = x.shape
    arrays = {
        "x_in": np.ascontiguousarray(x).reshape(batch, channels, height * width),
        "w_qkv_in": np.ascontiguousarray(L0_conv_w_qkv),
        "b_qkv_in": np.ascontiguousarray(L0_conv_b_qkv),
        "w_proj_in": np.ascontiguousarray(L0_conv_w_proj),
        "b_proj_in": np.ascontiguousarray(L0_conv_b_proj),
        "ident_in": np.eye(128, dtype=np.float32),
    }
    nc = bacc.Bacc("TRN2", target_bir_lowering=False, num_devices=1)
    ins = [nc.dram_tensor(n, a.shape, mybir.dt.from_np(a.dtype), kind="ExternalInput").ap()
           for n, a in arrays.items()]
    out = nc.dram_tensor("out", arrays["x_in"].shape, mybir.dt.float32, kind="ExternalOutput").ap()
    attention_kernel(nc, *ins, out)
    result = run_bass_kernel_spmd(nc, [arrays], core_ids=[0])
    return result.results[0]["out"].reshape(x.shape)
```
